# Optimizing a Trainium2 kernel written in Bass

```python
import numpy as np
import jax
import jax.numpy as jnp

def _softmax(x, axis=-1):
    return jax.nn.softmax(x, axis=axis)

def _gelu(x):
    return jax.nn.gelu(x, approximate=True)

def _silu(x):
    return jax.nn.silu(x)

def _sigmoid(x):
    return jax.nn.sigmoid(x)

def _layernorm(x, axis=-1, eps=1e-05):
    m = jnp.mean(x, axis=axis, keepdims=True)
    v = jnp.var(x, axis=axis, keepdims=True)
    return (x - m) / jnp.sqrt(v + eps)

def _scatter_add(tgt, idx, src, axis=0):
    return tgt.at[idx].add(src)

def _segment_sum(src, seg, n):
    return jax.ops.segment_sum(src, seg, n)
kernel_name = 'mk_recurrent_d1_jaxref_r8_2c53a2'

def setup_inputs(seed: int=0):
    np.random.seed(seed)
    _w = jnp.asarray

    def _L0_attn_setup():
        import jax, jax.numpy as jnp
        import numpy as np
        EMBED = 128
        HEADS = 16
        HEAD_DIM = EMBED // HEADS
        N, SEQ = (2, 256)
        key = jax.random.key(seed)
        ks = jax.random.split(key, 6)
        x = jax.random.normal(ks[0], (N, SEQ, EMBED), dtype=jnp.float32)
        s = 1.0 / np.sqrt(EMBED).astype(np.float32)
        Wv = jax.random.normal(ks[1], (EMBED, EMBED), dtype=jnp.float32) * s
        Wk = jax.random.normal(ks[2], (EMBED, EMBED), dtype=jnp.float32) * s
        Wq = jax.random.normal(ks[3], (EMBED, EMBED), dtype=jnp.float32) * s
        Wo = jax.random.normal(ks[4], (EMBED, EMBED), dtype=jnp.float32) * s
        bo = jax.random.normal(ks[5], (EMBED,), dtype=jnp.float32) * s
        return {'x': x, 'Wv': Wv, 'Wk': Wk, 'Wq': Wq, 'Wo': Wo, 'bo': bo}
    _L0_attn_in = _L0_attn_setup()

    def _L0_ffn_setup():
        import jax, jax.numpy as jnp
        import numpy as np
        DIM = 128
        DEPTH = 6
        HEADS = 16
        DIM_HEAD = 64
        WINDOW = 32
        INNER = HEADS * DIM_HEAD
        DIM_INNER = int(DIM * 4 * 2 / 3)
        QK_SCALE = 8.0

        def shift_tokens(t):
            a, s = jnp.split(t, 2, -1)
            s = jnp.pad(s, ((0, 0), (1, 0), (0, 0)))[:, :-1]
            return jnp.concatenate([a, s], -1)

        def l2norm(t):
            return t / jnp.maximum(jnp.linalg.norm(t, axis=-1, keepdims=True), 1e-12)

        def rotate_half(x):
            x1, x2 = jnp.split(x, 2, -1)
            return jnp.concatenate([-x2, x1], -1)

        def rotary_tables(n):
            half = jnp.arange(0, DIM_HEAD, 2, dtype=jnp.float32)
            inv_freq = 1.0 / 10000.0 ** (half / DIM_HEAD)
            t = jnp.arange(n, dtype=jnp.float32)
            freqs = t[:, None] * inv_freq[None, :]
            freqs = jnp.concatenate([freqs, freqs], -1)
            base_scale = (half + 0.4 * DIM_HEAD) / (1.4 * DIM_HEAD)
            power = (t - n // 2) / (WINDOW // 2)
            scale = base_scale[None, :] ** power[:, None]
            scale = jnp.concatenate([scale, scale], -1)
            return (freqs, scale)

        def local_attention(q, k, v):
            b, h, n, d = q.shape
            w = WINDOW
            nw = n // w
            bq = q.reshape(b, h, nw, w, d)
            bk = k.reshape(b, h, nw, w, d)
            bv = v.reshape(b, h, nw, w, d)

            def look(t):
                p = jnp.pad(t, ((0, 0), (0, 0), (1, 0), (0, 0), (0, 0)))
                return jnp.concatenate([p[:, :, :nw], p[:, :, 1:]], axis=3)
            bk2, bv2 = (look(bk), look(bv))
            seq = jnp.arange(n).reshape(nw, w)
            seq_p = jnp.pad(seq, ((1, 0), (0, 0)), constant_values=-1)
            jt = jnp.concatenate([seq_p[:nw], seq_p[1:]], axis=1)
            it = seq[:, :, None]
            jb = jt[:, None, :]
            mask = (it < jb) | (it > jb + w) | (jb == -1)
            sim = jnp.einsum('bhwie,bhwje->bhwij', bq, bk2) * QK_SCALE
            sim = jnp.where(mask, -jnp.finfo(sim.dtype).max, sim)
            attn = jax.nn.softmax(sim, -1)
            out = jnp.einsum('bhwij,bhwje->bhwie', attn, bv2)
            return out.reshape(b, h, n, d)

        def attn_layer(x, Wqkv, qs, ksc, Wo):
            b, n, _ = x.shape
            qkv = x @ Wqkv
            q, k, v = jnp.split(qkv, 3, -1)
            sh = lambda t: t.reshape(b, n, HEADS, DIM_HEAD).transpose(0, 2, 1, 3)
            q, k, v = (sh(q), sh(k), sh(v))
            q = l2norm(q) * qs
            k = l2norm(k) * ksc
            freqs, scale = rotary_tables(n)
            cos, sin = (jnp.cos(freqs), jnp.sin(freqs))
            q = q * cos * scale + rotate_half(q) * sin * scale
            inv = 1.0 / scale
            k = k * cos * inv + rotate_half(k) * sin * inv
            out = local_attention(q, k, v)
            out = out.transpose(0, 2, 1, 3).reshape(b, n, INNER)
            return out @ Wo

        def ffn_layer(x, g, bln, W1, b1, W2, b2):
            mu = x.mean(-1, keepdims=True)
            var = ((x - mu) ** 2).mean(-1, keepdims=True)
            xn = (x - mu) / jnp.sqrt(var + 1e-05) * g + bln
            hg = xn @ W1 + b1
            a, gate = jnp.split(hg, 2, -1)
            return a * jax.nn.gelu(gate, approximate=False) @ W2 + b2
        key = jax.random.key(seed)
        ks = jax.random.split(key, 8)
        B, N = (2, 256)
        init = lambda k, shape: jax.random.normal(k, shape, jnp.float32) * 0.02
        return {'x': jax.random.normal(ks[0], (B, N, DIM), jnp.float32), 'Wqkv': init(ks[1], (DEPTH, DIM, 3 * INNER)), 'q_scale': jnp.ones((DEPTH, DIM_HEAD), jnp.float32), 'k_scale': jnp.ones((DEPTH, DIM_HEAD), jnp.float32), 'Wo': init(ks[2], (DEPTH, INNER, DIM)), 'ln_g': jnp.ones((DEPTH, DIM), jnp.float32), 'ln_b': jnp.zeros((DEPTH, DIM), jnp.float32), 'W1': init(ks[3], (DEPTH, DIM, 2 * DIM_INNER)), 'b1': jnp.zeros((DEPTH, 2 * DIM_INNER), jnp.float32), 'W2': init(ks[4], (DEPTH, DIM_INNER, DIM)), 'b2': jnp.zeros((DEPTH, DIM), jnp.float32)}
    _L0_ffn_in = _L0_ffn_setup()
    _d = {'L0_attn_x': _L0_attn_in['x'], 'L0_attn_Wv': _L0_attn_in['Wv'], 'L0_attn_Wk': _L0_attn_in['Wk'], 'L0_attn_Wq': _L0_attn_in['Wq'], 'L0_attn_Wo': _L0_attn_in['Wo'], 'L0_attn_bo': _L0_attn_in['bo'], 'L0_ffn_Wqkv': _L0_ffn_in['Wqkv'], 'L0_ffn_q_scale': _L0_ffn_in['q_scale'], 'L0_ffn_k_scale': _L0_ffn_in['k_scale'], 'L0_ffn_Wo': _L0_ffn_in['Wo'], 'L0_ffn_ln_g': _L0_ffn_in['ln_g'], 'L0_ffn_ln_b': _L0_ffn_in['ln_b'], 'L0_ffn_W1': _L0_ffn_in['W1'], 'L0_ffn_b1': _L0_ffn_in['b1'], 'L0_ffn_W2': _L0_ffn_in['W2'], 'L0_ffn_b2': _L0_ffn_in['b2']}
    _x0 = _d['L0_attn_x']
    _d['L0_attn_x'] = jax.random.normal(jax.random.fold_in(jax.random.key(seed), 1), (1, 2048, 128), dtype=_x0.dtype)
    del _x0
    return _d

def reference(L0_attn_x, L0_attn_Wv, L0_attn_Wk, L0_attn_Wq, L0_attn_Wo, L0_attn_bo, L0_ffn_Wqkv, L0_ffn_q_scale, L0_ffn_k_scale, L0_ffn_Wo, L0_ffn_ln_g, L0_ffn_ln_b, L0_ffn_W1, L0_ffn_b1, L0_ffn_W2, L0_ffn_b2):

    def _L0_attn_ref(x, Wv, Wk, Wq, Wo, bo):
        import jax, jax.numpy as jnp
        import numpy as np
        EMBED = 128
        HEADS = 16
        HEAD_DIM = EMBED // HEADS
        N, SEQ = (2, 256)
        n, s, e = x.shape
        h, d = (HEADS, e // HEADS)
        values = (x @ Wv).reshape(n, s, h, d)
        keys = (x @ Wk).reshape(n, s, h, d)
        queries = (x @ Wq).reshape(n, s, h, d)
        energy = jnp.einsum('nqhd,nkhd->nqkh', queries, keys)
        attention = jax.nn.softmax(energy / np.sqrt(d).astype(np.float32), axis=2)
        out = jnp.einsum('nqkh,nkhd->nqhd', attention, values)
        out = out.reshape(n, s, e)
        return out @ Wo + bo

    def _L0_ffn_ref(x, Wqkv, q_scale, k_scale, Wo, ln_g, ln_b, W1, b1, W2, b2):
        import jax, jax.numpy as jnp
        import numpy as np
        DIM = 128
        DEPTH = 6
        HEADS = 16
        DIM_HEAD = 64
        WINDOW = 32
        INNER = HEADS * DIM_HEAD
        DIM_INNER = int(DIM * 4 * 2 / 3)
        QK_SCALE = 8.0

        def shift_tokens(t):
            a, s = jnp.split(t, 2, -1)
            s = jnp.pad(s, ((0, 0), (1, 0), (0, 0)))[:, :-1]
            return jnp.concatenate([a, s], -1)

        def l2norm(t):
            return t / jnp.maximum(jnp.linalg.norm(t, axis=-1, keepdims=True), 1e-12)

        def rotate_half(x):
            x1, x2 = jnp.split(x, 2, -1)
            return jnp.concatenate([-x2, x1], -1)

        def rotary_tables(n):
            half = jnp.arange(0, DIM_HEAD, 2, dtype=jnp.float32)
            inv_freq = 1.0 / 10000.0 ** (half / DIM_HEAD)
            t = jnp.arange(n, dtype=jnp.float32)
            freqs = t[:, None] * inv_freq[None, :]
            freqs = jnp.concatenate([freqs, freqs], -1)
            base_scale = (half + 0.4 * DIM_HEAD) / (1.4 * DIM_HEAD)
            power = (t - n // 2) / (WINDOW // 2)
            scale = base_scale[None, :] ** power[:, None]
            scale = jnp.concatenate([scale, scale], -1)
            return (freqs, scale)

        def local_attention(q, k, v):
            b, h, n, d = q.shape
            w = WINDOW
            nw = n // w
            bq = q.reshape(b, h, nw, w, d)
            bk = k.reshape(b, h, nw, w, d)
            bv = v.reshape(b, h, nw, w, d)

            def look(t):
                p = jnp.pad(t, ((0, 0), (0, 0), (1, 0), (0, 0), (0, 0)))
                return jnp.concatenate([p[:, :, :nw], p[:, :, 1:]], axis=3)
            bk2, bv2 = (look(bk), look(bv))
            seq = jnp.arange(n).reshape(nw, w)
            seq_p = jnp.pad(seq, ((1, 0), (0, 0)), constant_values=-1)
            jt = jnp.concatenate([seq_p[:nw], seq_p[1:]], axis=1)
            it = seq[:, :, None]
            jb = jt[:, None, :]
            mask = (it < jb) | (it > jb + w) | (jb == -1)
            sim = jnp.einsum('bhwie,bhwje->bhwij', bq, bk2) * QK_SCALE
            sim = jnp.where(mask, -jnp.finfo(sim.dtype).max, sim)
            attn = jax.nn.softmax(sim, -1)
            out = jnp.einsum('bhwij,bhwje->bhwie', attn, bv2)
            return out.reshape(b, h, n, d)

        def attn_layer(x, Wqkv, qs, ksc, Wo):
            b, n, _ = x.shape
            qkv = x @ Wqkv
            q, k, v = jnp.split(qkv, 3, -1)
            sh = lambda t: t.reshape(b, n, HEADS, DIM_HEAD).transpose(0, 2, 1, 3)
            q, k, v = (sh(q), sh(k), sh(v))
            q = l2norm(q) * qs
            k = l2norm(k) * ksc
            freqs, scale = rotary_tables(n)
            cos, sin = (jnp.cos(freqs), jnp.sin(freqs))
            q = q * cos * scale + rotate_half(q) * sin * scale
            inv = 1.0 / scale
            k = k * cos * inv + rotate_half(k) * sin * inv
            out = local_attention(q, k, v)
            out = out.transpose(0, 2, 1, 3).reshape(b, n, INNER)
            return out @ Wo

        def ffn_layer(x, g, bln, W1, b1, W2, b2):
            mu = x.mean(-1, keepdims=True)
            var = ((x - mu) ** 2).mean(-1, keepdims=True)
            xn = (x - mu) / jnp.sqrt(var + 1e-05) * g + bln
            hg = xn @ W1 + b1
            a, gate = jnp.split(hg, 2, -1)
            return a * jax.nn.gelu(gate, approximate=False) @ W2 + b2
        for i in range(DEPTH):
            x = attn_layer(shift_tokens(x), Wqkv[i], q_scale[i], k_scale[i], Wo[i]) + x
            x = ffn_layer(shift_tokens(x), ln_g[i], ln_b[i], W1[i], b1[i], W2[i], b2[i]) + x
        return x
    x = L0_attn_x
    xn = _layernorm(x, axis=-1)
    s = _L0_attn_ref(xn, L0_attn_Wv, L0_attn_Wk, L0_attn_Wq, L0_attn_Wo, L0_attn_bo)
    g = _silu(_L0_ffn_ref(xn, L0_ffn_Wqkv, L0_ffn_q_scale, L0_ffn_k_scale, L0_ffn_Wo, L0_ffn_ln_g, L0_ffn_ln_b, L0_ffn_W1, L0_ffn_b1, L0_ffn_W2, L0_ffn_b2))
    x = x + s * g
    return x

_drawn_inputs = setup_inputs


def setup_inputs(seed=0):
    import zlib

    import numpy as np

    out = dict(_drawn_inputs(seed))
    spreads = {'L0_ffn_q_scale': (1.0, 0.2),
     'L0_ffn_k_scale': (1.0, 0.2),
     'L0_ffn_ln_g': (1.0, 0.2),
     'L0_ffn_ln_b': (0.0, 0.1),
     'L0_ffn_b1': (0.0, 0.1),
     'L0_ffn_b2': (0.0, 0.1)}
    factors = {}
    for name, (base, spread) in spreads.items():
        noise = np.random.default_rng([zlib.crc32(name.encode()), seed]).standard_normal(out[name].shape)
        drawn = base * np.exp(spread * noise) if base else spread * noise
        out[name] = jnp.asarray(drawn.astype(out[name].dtype))
    for name, factor in factors.items():
        out[name] = (out[name] * factor).astype(out[name].dtype)
    return out
```

```python
from contextlib import ExitStack

import numpy as np

import concourse.bass as bass
from concourse import mybir

F32 = mybir.dt.float32
F32R = mybir.dt.float32r
BF16 = mybir.dt.bfloat16
ALU = mybir.AluOpType
ACT = mybir.ActivationFunctionType
AX = mybir.AxisListType

P = 128
SEQ = 2048
DIM = 128
TILES = SEQ // P
BANK = 512

GH = 16
GD = DIM // GH
SPLIT = 4 * GD
GBUF = 4
LEAD = 20
PSLOTS = 8
PVB = 2
VCOL = 32

DEPTH = 6
NH = 16
HD = 64
PAIRS = NH // 2
WIN = 32
NWIN = P // WIN
KEYS = 2 * WIN
INNER = NH * HD
FF = int(DIM * 4 * 2 / 3)
FFT = 3
FFL = FF - (FFT - 1) * P
STEPS = DEPTH * TILES
EPS = 1e-5
LAST = 4


def need(eng, sem, value):
    if not isinstance(value, int) or value > 0:
        eng.wait_ge(sem, value)


def layer_of(n):
    l = n // TILES if isinstance(n, int) else (n >> 4)
    return l if isinstance(n, int) else l.with_bounds(min_val=0, max_val=DEPTH - 1)


def build(nc, x, wv, wk, wq, wo, bo, lqkv, lqs, lks, lwo, lg, lb, lw1, lb1, lw2, lb2,
          rope, carry_scale, mask, eye, out):
    scratch = nc.dram_tensor("split_operands", [4, DIM, SEQ], F32, kind="Internal").ap()
    max_scratch = nc.dram_tensor("maxima", [2, TILES, P], F32, kind="Internal").ap()
    persistent = ExitStack()

    def keep(name, shape, dt=F32):
        return persistent.enter_context(nc.sbuf_tensor(name, shape, dt))

    with persistent:
        ident = keep("ident", [P, P])
        X = keep("X", [P, 1 + SEQ])
        att = keep("att", [P, SEQ])
        with ExitStack() as ctx:
            vtok = ctx.enter_context(nc.sbuf_tensor("vtok", [P, TILES, DIM], F32))
            otok = ctx.enter_context(nc.sbuf_tensor("otok", [P, TILES, DIM], F32))
            wout = ctx.enter_context(nc.sbuf_tensor("wout", [P, DIM], F32))
            bout = ctx.enter_context(nc.sbuf_tensor("bout", [P, 1], F32))
            stage_a(nc, x, wq, wk, wv, wo, bo, eye, scratch, ident, X, vtok, wout, bout)
            stage_b(nc, scratch, max_scratch, ident, vtok, otok)
            stage_c(nc, ident, otok, wout, bout, att)
        stage_d(nc, lqkv, lqs, lks, lwo, lg, lb, lw1, lb1, lw2, lb2, rope, carry_scale, mask, ident, X)
        stage_e(nc, x, ident, X, att, out)


def stage_a(nc, x, wq, wk, wv, wo, bo, eye, scratch, ident, X, vtok, wout, bout):
    with ExitStack() as ctx:
        def sb(name, shape, dt=F32):
            return ctx.enter_context(nc.sbuf_tensor(name, shape, dt))

        def sem(name):
            return ctx.enter_context(nc.semaphore(name))

        xin = sb("xin", [P, TILES, DIM])
        xc = sb("xc", [P, TILES, DIM])
        sq = sb("sq", [P, TILES, DIM])
        mean = sb("mean", [P, TILES])
        std = sb("std", [P, TILES])
        rstd = sb("rstd", [P, TILES])
        w = sb("w_in", [P, 3, DIM])
        split = sb("split", [P, 4, SEQ], F32R)
        ps = ctx.enter_context(nc.psum_tensor("psA", [P, 8, BANK], F32))

        x_in, w_in, cst_in, stored = sem("x_in"), sem("w_in_s"), sem("cst_in"), sem("stored")
        v_sum, v_mean, v_xc, v_var, v_rstd, v_xn = (sem(f"v_{n}") for n in ("sum", "mean", "xc", "var", "rstd", "xn"))
        a_sq, p_xt, a_xt, p_qk, v_hi, v_lo, p_v, a_v = (
            sem(n) for n in ("a_sq", "p_xt", "a_xt", "p_qk", "v_hi", "v_lo", "p_v", "a_v"))
        g_zero, a_std = sem("g_zero"), sem("a_std")

        block = ctx.enter_context(nc.Block())

        @block.sync
        def _(sp):
            sp.dma_start(xin[:], x[0].rearrange("(t p) d -> p t d", p=P)).then_inc(x_in, 16)
            sp.dma_start(ident[:], eye).then_inc(cst_in, 16)
            for n, src in enumerate((wq, wk, wv)):
                sp.dma_start(w[:, n, :], src).then_inc(w_in, 16)
            sp.dma_start(wout[:], wo).then_inc(cst_in, 16)
            sp.dma_start(bout[:], bo.rearrange("(d a) -> d a", a=1)).then_inc(cst_in, 16)
            for n in range(4):
                sp.wait_ge(v_hi if n % 2 == 0 else v_lo, 4 * (n // 2 + 1))
                sp.dma_start(scratch[n], split[:, n, :].bitcast(F32)).then_inc(stored, 16)
            sp.wait_ge(stored, 64)

        @block.gpsimd
        def _(pool):
            pool.memset(X[:, 0:1], 0.0).then_inc(g_zero, 1)

        @block.vector
        def _(dve):
            dve.wait_ge(x_in, 16)
            dve.tensor_reduce(mean[:], xin[:], AX.X, ALU.add).then_inc(v_sum, 1)
            dve.wait_ge(v_sum, 1)
            dve.tensor_scalar(mean[:], mean[:], 1.0 / DIM, None, ALU.mult).then_inc(v_mean, 1)
            dve.wait_ge(v_mean, 1)
            dve.tensor_tensor(xc[:], xin[:], mean[:].unsqueeze(2).broadcast_to([P, TILES, DIM]),
                              ALU.subtract).then_inc(v_xc, 1)
            dve.wait_ge(a_sq, 1)
            dve.tensor_reduce(rstd[:], sq[:], AX.X, ALU.add).then_inc(v_var, 1)
            dve.wait_ge(v_var, 1)
            dve.tensor_scalar(rstd[:], rstd[:], 1.0 / DIM, EPS, ALU.mult, ALU.add).then_inc(v_rstd, 1)
            dve.wait_ge(a_std, 1)
            dve.reciprocal(rstd[:], std[:]).then_inc(v_rstd, 1)
            dve.wait_ge(v_rstd, 2)
            dve.tensor_tensor(xc[:], xc[:], rstd[:].unsqueeze(2).broadcast_to([P, TILES, DIM]),
                              ALU.mult).then_inc(v_xn, 1)
            for m in range(8):
                n, c = m // 4, m % 4
                dve.wait_ge(p_qk, m + 1)
                hi, lo = split[:, 2 * n, c * BANK:(c + 1) * BANK], split[:, 2 * n + 1, c * BANK:(c + 1) * BANK]
                dve.tensor_copy(hi, ps[:, m, :]).then_inc(v_hi, 1)
                dve.wait_ge(v_hi, m + 1)
                dve.tensor_tensor(lo, ps[:, m, :], hi.bitcast(F32), ALU.subtract).then_inc(v_lo, 1)

        @block.scalar
        def _(act):
            act.wait_ge(v_xc, 1)
            act.activation(sq[:], xc[:], ACT.Square).then_inc(a_sq, 1)
            act.wait_ge(v_rstd, 1)
            act.activation(std[:], rstd[:], ACT.Sqrt).then_inc(a_std, 1)
            for c in range(4):
                act.wait_ge(p_xt, c + 1)
                act.activation(X[:, 1 + c * BANK:1 + (c + 1) * BANK], ps[:, c, :], ACT.Copy).then_inc(a_xt, 1)
            for c in range(4):
                act.wait_ge(p_v, c + 1)
                act.activation(vtok[:, 4 * c:4 * c + 4, :], ps[:, c, :].rearrange("p (t d) -> p t d", t=4),
                               ACT.Copy).then_inc(a_v, 1)

        @block.tensor
        def _(pe):
            pe.wait_ge(cst_in, 48)
            pe.wait_ge(v_xn, 1)
            for t in range(TILES):
                last = pe.transpose(ps[:, t // 4, t % 4 * P:(t % 4 + 1) * P], xc[:, t, :], ident[:])
                if t % 4 == 3:
                    last.then_inc(p_xt, 1)
            pe.wait_ge(w_in, 48)
            pe.wait_ge(a_xt, 4)
            for m in range(8):
                n, c = m // 4, m % 4
                pe.matmul(ps[:, m, :], w[:, n, :], X[:, 1 + c * BANK:1 + (c + 1) * BANK],
                          start=True, stop=True).then_inc(p_qk, 1)
            for t in range(TILES):
                if t % 4 == 0:
                    pe.wait_ge(v_lo, t // 4 + 1)
                last = pe.matmul(ps[:, t // 4, t % 4 * P:(t % 4 + 1) * P], X[:, 1 + t * P:1 + (t + 1) * P],
                                 w[:, 2, :], start=True, stop=True)
                if t % 4 == 3:
                    last.then_inc(p_v, 1)


def stage_b(nc, scratch, max_scratch, ident, vtok, otok):
    WARM = 8
    TOTAL = GH * TILES
    with ExitStack() as ctx:
        def sb(name, shape, dt=F32):
            return ctx.enter_context(nc.sbuf_tensor(name, shape, dt))

        def pb(name, shape):
            return ctx.enter_context(nc.psum_tensor(name, shape, F32))

        def sem(name):
            return ctx.enter_context(nc.semaphore(name))

        qs = sb("qs", [P, GBUF, SEQ], F32R)
        ks = sb("ks", [P, GBUF, SEQ], F32R)
        zero2 = sb("zero2", [2, SEQ], F32R)
        vs = sb("vs", [P, 2, TILES, VCOL])
        prob = sb("prob", [P, PSLOTS, SEQ])
        part = sb("part", [P, 2, TILES, 4])
        nmax = sb("nmax", [P, TILES])
        nmax_hi = sb("nmax_hi", [TILES, P], F32R)
        nmax_lo = sb("nmax_lo", [TILES, P], F32R)
        oacc = sb("oacc", [P, BANK])
        rden = sb("rden", [P, 4, 4])
        ps_max = pb("ps_max", [P, 2, BANK])
        ps_exp = pb("ps_exp", [P, 2, 2 * BANK])
        ps_o = pb("ps_o", [P, BANK])
        ps_misc = pb("ps_misc", [P, BANK])

        loaded = [sem(f"loaded{b}") for b in range(GBUF)]
        max_out, max_rows = sem("max_out"), sem("max_rows")
        g_init, v_init, g_vs = sem("g_init"), sem("v_init"), sem("g_vs")
        p_max, v_red, v_nmax, p_maxt, v_mhi, v_mlo = (
            sem(n) for n in ("p_max", "v_red", "v_nmax", "p_maxt", "v_mhi", "v_mlo"))
        p_exp, a_exp, p_pv, a_oacc, p_ot, v_rden, v_otok = (
            sem(n) for n in ("p_exp", "a_exp", "p_pv", "a_oacc", "p_otr", "v_rdenB", "v_otok"))
        LOADS = 9

        block = ctx.enter_context(nc.Block())

        def walk(eng, step):
            for w in range(WARM):
                step(w, w, 0)
            with eng.Fori(0, 3) as g:
                for k in range(WARM, WARM + 4 * TILES):
                    step(g * (4 * TILES) + k, k, g)
            for w in range(WARM + 12 * TILES, TOTAL):
                step(w, w, 0)

        @block.sync
        def _(sp):
            def load(h, b):
                rows = bass.ds(h * GD, GD)
                for r, (qn, kn) in enumerate(((0, 2), (0, 3), (1, 2), (1, 3))):
                    sp.dma_start(qs[r * GD:(r + 1) * GD, b, :].bitcast(F32), scratch[qn, rows, :]).then_inc(loaded[b], 16)
                    sp.dma_start(ks[r * GD:(r + 1) * GD, b, :].bitcast(F32), scratch[kn, rows, :]).then_inc(loaded[b], 16)
                sp.dma_start(qs[SPLIT:SPLIT + 2, b, :].bitcast(F32), zero2[:].bitcast(F32)).then_inc(loaded[b], 16)

            def put_max(h, b):
                sp.wait_ge(v_mlo, h + 1)
                for r, src in ((0, nmax_hi), (1, nmax_lo)):
                    sp.dma_start(max_scratch[r], src[:].bitcast(F32)).then_inc(max_out, 16)
                sp.wait_ge(max_out, h * 32 + 32)
                sp.dma_start(qs[SPLIT:SPLIT + 2, b, :].bitcast(F32),
                             max_scratch.rearrange("r t q -> r (t q)")).then_inc(max_rows, 16)

            sp.wait_ge(g_init, 3)
            sp.wait_ge(v_init, 4)
            for h in range(GBUF):
                load(h, h)
            put_max(0, 0)

            def head(h, k):
                put_max(h, k % GBUF)
                sp.wait_ge(p_exp, 2 * TILES * h)
                sp.wait_ge(p_pv, (TILES // PVB) * (h - 1) + 1) if k > 1 else None
                load(h + GBUF - 1, (k - 1) % GBUF)

            with sp.Fori(0, 3) as g:
                for k in range(1, 5):
                    head(g * 4 + k, k)
            for h in range(13, GH):
                put_max(h, h % GBUF)
            sp.wait_ge(max_rows, 16 * GH)

        @block.gpsimd
        def _(pool):
            pool.memset(zero2[:].bitcast(F32), 0.0).then_inc(g_init, 1)
            pool.memset(vs[:], 0.0).then_inc(g_init, 1)
            pool.wait_ge(g_init, 2)
            pool.memset(vs[:, :, :, GD:GD + 1], 1.0).then_inc(g_init, 1)
            pool.wait_ge(g_init, 3)

            def values(h, b):
                pool.tensor_copy(vs[:, b, :, 0:GD], vtok[:, :, bass.ds(h * GD, GD)]).then_inc(g_vs, 1)

            values(0, 0)
            values(1, 1)
            with pool.Fori(1, GH // 2) as hh:
                for b in range(2):
                    pool.wait_ge(p_pv, (TILES // PVB) * (hh * 2 + b - 1))
                    values(hh * 2 + b, b)

        @block.vector
        def _(dve):
            for b in range(GBUF):
                dve.memset(qs[:, b, :].bitcast(F32), 0.0)
                dve.memset(ks[:, b, :].bitcast(F32), 0.0).then_inc(v_init, 1)
            dve.wait_ge(v_init, 4)
            dve.memset(ks[SPLIT:SPLIT + 2, :, :].bitcast(F32), 1.0).then_inc(v_init, 1)

            def reduce_tile(u, ku):
                t, b = ku % TILES, ku // TILES % 2
                for c in range(4):
                    dve.wait_ge(p_max, u * 4 + c + 1)
                    dve.tensor_reduce(part[:, b, t, c:c + 1], ps_max[:, c % 2, :], AX.X, ALU.max).then_inc(v_red, 1)
                if t == TILES - 1:
                    dve.wait_ge(v_red, u * 4 + 4)
                    if ku >= TILES:
                        dve.wait_ge(p_maxt, (u - (TILES - 1)) // TILES)
                    dve.tensor_reduce(nmax[:], part[:, b], AX.X, ALU.max, negate=True).then_inc(v_nmax, 1)

            def split_max(h, first):
                dve.wait_ge(p_maxt, h + 1)
                if not first:
                    dve.wait_ge(max_rows, h * 16)
                dve.tensor_copy(nmax_hi[:], ps_misc[0:TILES, 0:P]).then_inc(v_mhi, 1)
                dve.wait_ge(v_mhi, h + 1)
                dve.tensor_tensor(nmax_lo[:], ps_misc[0:TILES, 0:P], nmax_hi[:].bitcast(F32),
                                  ALU.subtract).then_inc(v_mlo, 1)

            def finish_head(h):
                dve.wait_ge(p_ot, h + 1)
                o = ps_misc[:].rearrange("p (s c m) -> p c s m", s=4, c=4)
                dve.reciprocal(rden[:], o[:, :, :, GD]).then_inc(v_rden, 1)
                dve.wait_ge(v_rden, h + 1)
                dve.tensor_tensor(otok[:, :, bass.ds(h * GD, GD)].rearrange("p (c s) d -> p c s d", c=4),
                                  o[:, :, :, 0:GD], rden[:].unsqueeze(3).broadcast_to([P, 4, 4, GD]),
                                  ALU.mult).then_inc(v_otok, 1)

            for u in range(LEAD):
                reduce_tile(u, u)
                if u == TILES + 1:
                    split_max(0, True)

            def step(w, k, lead):
                if not (isinstance(w, int) and w + LEAD >= TOTAL):
                    reduce_tile(w + LEAD, k + LEAD)
                if k % TILES == 1 and k > 1:
                    finish_head(lead * 4 + (k // TILES - 1))
                if k % TILES == 13 and k < TOTAL - TILES:
                    split_max(lead * 4 + (k // TILES + 1), False)

            walk(dve, step)
            finish_head(GH - 1)

        @block.scalar
        def _(act):
            def step(w, k, lead):
                for half in range(2):
                    act.wait_ge(p_exp, w * 2 + half + 1)
                    if k >= PSLOTS:
                        act.wait_ge(p_pv, lead * (4 * TILES // PVB) + (k // PVB - PSLOTS // PVB + 1))
                    act.activation(prob[:, k % PSLOTS, half * 2 * BANK:(half + 1) * 2 * BANK],
                                   ps_exp[:, half, :], ACT.Exp, scale=GD ** -0.5).then_inc(a_exp, 1)
                if k % TILES == 0 and k > 0:
                    save_o(lead * 4 + (k // TILES - 1), k > TILES)

            def save_o(h, later):
                act.wait_ge(p_pv, (h + 1) * (TILES // PVB))
                if later:
                    act.wait_ge(p_ot, h)
                act.activation(oacc[:], ps_o[:], ACT.Copy).then_inc(a_oacc, 1)

            walk(act, step)
            save_o(GH - 1, True)

        @block.tensor
        def _(pe):
            pe.wait_ge(v_init, 5)

            def max_scores(u, ku, c):
                b, t, n = ku // TILES % GBUF, ku % TILES, u * 4 + c
                if t == 0 and c == 0:
                    pe.wait_ge(loaded[b], ((u - ku % (GBUF * TILES)) // (GBUF * TILES) + 1) * (LOADS * 16))
                if ku > 0 or c >= 2:
                    pe.wait_ge(v_red, n - 1)
                pe.matmul(ps_max[:, c % 2, :], qs[:, b, t * P:(t + 1) * P], ks[:, b, c * BANK:(c + 1) * BANK],
                          start=True, stop=True).then_inc(p_max, 1)

            def turn_max(h, first):
                pe.wait_ge(v_nmax, h + 1)
                if not first:
                    pe.wait_ge(v_otok, h - 1) if not isinstance(h, int) or h > 1 else None
                pe.transpose(ps_misc[0:TILES, 0:P], nmax[:], ident[:]).then_inc(p_maxt, 1)

            def turn_o(h):
                pe.wait_ge(a_oacc, h + 1)
                if isinstance(h, int) and h + 2 > GH:
                    pe.wait_ge(v_otok, h)
                else:
                    pe.wait_ge(v_mlo, h + 2)
                for s in range(4):
                    last = pe.transpose(ps_misc[:, s * P:(s + 1) * P], oacc[:, s * P:(s + 1) * P], ident[:])
                last.then_inc(p_ot, 1)

            def exp_scores(w, k, half):
                b, t = k // TILES % GBUF, k % TILES
                if t == 0 and half == 0:
                    pe.wait_ge(max_rows, (w // TILES + 1) * 16)
                if k > 0:
                    pe.wait_ge(a_exp, w * 2 + half - 1)
                for cc in range(2):
                    last = pe.matmul(ps_exp[:, half, cc * BANK:(cc + 1) * BANK], ks[:, b, t * P:(t + 1) * P],
                                     qs[:, b, (2 * half + cc) * BANK:(2 * half + cc + 1) * BANK],
                                     start=True, stop=True)
                last.then_inc(p_exp, 1)

            def value_products(w, k):
                kk = k - PVB
                h = kk // TILES
                if kk % TILES == 0:
                    pe.wait_ge(g_vs, (w - PVB) // TILES + 1)
                    if kk >= TILES:
                        pe.wait_ge(a_oacc, (w - PVB) // TILES)
                pe.wait_ge(a_exp, w * 2)
                for m in range(PVB):
                    t = (kk + m) % TILES
                    for c in range(4):
                        last = pe.matmul(ps_o[32 * c:32 * c + VCOL, :], vs[:, h % 2, t, :],
                                         prob[:, (kk + m) % PSLOTS, c * BANK:(c + 1) * BANK],
                                         start=(t == 0), stop=(t == TILES - 1), skip_group_check=True)
                last.then_inc(p_pv, 1)

            for u in range(LEAD):
                for c in range(4):
                    max_scores(u, u, c)
                if u == TILES + 1:
                    turn_max(0, True)

            def step(w, k, lead):
                ahead = not (isinstance(w, int) and w + LEAD >= TOTAL)
                for half in range(2):
                    exp_scores(w, k, half)
                    if ahead:
                        max_scores(w + LEAD, k + LEAD, 2 * half)
                        max_scores(w + LEAD, k + LEAD, 2 * half + 1)
                if k % PVB == 0 and k > 0:
                    value_products(w, k)
                if k % TILES == 1 and k > 1:
                    turn_o(lead * 4 + (k // TILES - 1))
                if k % TILES == 13 and k < TOTAL - TILES:
                    turn_max(lead * 4 + (k // TILES + 1), False)

            walk(pe, step)
            value_products(TOTAL, TOTAL)
            turn_o(GH - 1)


def stage_c(nc, ident, otok, wout, bout, att):
    with ExitStack() as ctx:
        def sem(name):
            return ctx.enter_context(nc.semaphore(name))

        ot = ctx.enter_context(nc.sbuf_tensor("ot", [P, SEQ], F32))
        ps = ctx.enter_context(nc.psum_tensor("psC", [P, 8, BANK], F32))
        p_t, a_t, p_w, v_w = sem("p_t"), sem("a_t"), sem("p_w"), sem("v_w")
        block = ctx.enter_context(nc.Block())

        @block.tensor
        def _(pe):
            for t in range(TILES):
                last = pe.transpose(ps[:, t // 4, t % 4 * P:(t % 4 + 1) * P], otok[:, t, :], ident[:])
                if t % 4 == 3:
                    last.then_inc(p_t, 1)
            for c in range(4):
                pe.wait_ge(a_t, c + 1)
                pe.matmul(ps[:, 4 + c, :], wout[:], ot[:, c * BANK:(c + 1) * BANK],
                          start=True, stop=True).then_inc(p_w, 1)

        @block.scalar
        def _(act):
            for c in range(4):
                act.wait_ge(p_t, c + 1)
                act.activation(ot[:, c * BANK:(c + 1) * BANK], ps[:, c, :], ACT.Copy).then_inc(a_t, 1)

        @block.vector
        def _(dve):
            for c in range(4):
                dve.wait_ge(p_w, c + 1)
                dve.tensor_scalar(att[:, c * BANK:(c + 1) * BANK], ps[:, 4 + c, :], bout[:, 0:1], None,
                                  ALU.add).then_inc(v_w, 1)
            dve.wait_ge(v_w, 4)


def stage_d(nc, lqkv, lqs, lks, lwo, lg, lb, lw1, lb1, lw2, lb2, rope, carry_scale, mask, ident, X):
    with ExitStack() as ctx:
        def sb(name, shape, dt=F32):
            return ctx.enter_context(nc.sbuf_tensor(name, shape, dt))

        def sem(name):
            return ctx.enter_context(nc.semaphore(name))

        wqkv = sb("wqkv", [P, 3 * INNER])
        wo_sb = sb("wo_sb", [P, PAIRS, DIM])
        w1_sb = sb("w1_sb", [P, 2, FFT * P])
        w2_sb = sb("w2_sb", [P, FFT, DIM])
        scales = sb("scales", [P, DEPTH, 4, HD])
        gcol = sb("gcol", [P, DEPTH])
        bcol = sb("bcol", [P, DEPTH])
        b2col = sb("b2col", [P, DEPTH])
        b1col = sb("b1col", [P, 2, FFT, DEPTH])
        rope_sb = sb("rope_sb", [P, TILES, 4, HD])
        cscale = sb("cscale", [P, 1])
        mask_f = sb("mask_f", [P, 2, KEYS])
        mask_b = sb("mask_b", [P, 2, KEYS], BF16)
        ident_b = sb("ident_b", [P, P], BF16)
        mean_w = sb("mean_w", [P, P])
        eps = sb("eps", [P, 1])
        Y = sb("Y", [P, 1 + SEQ])
        xs = sb("xs", [P, P])
        ys = sb("ys", [P, P])
        tab = sb("tab", [P, 4, HD])
        rot = sb("rot", [P, 2, INNER])
        rot2 = sb("rot2", [P, 2, INNER])
        sq = sb("sqD", [P, 2, INNER])
        ssum = sb("ssum", [P, 2, NH])
        clamped = sb("clamped", [P, 2, NH])
        norm = sb("norm", [P, 2, NH])
        rnorm = sb("rnorm", [P, 2, NH])
        qT = sb("qT", [P, PAIRS, P])
        kT = sb("kT", [P, PAIRS, 2, WIN + P])
        vtile = sb("vtile", [P, 4, INNER])
        vwin = sb("vwin", [P, NWIN, 2, PAIRS, HD])
        mx = sb("mx", [P, NH])
        shifted = sb("shifted", [P, NH * KEYS])
        prob = sb("probD", [P, NH * KEYS])
        den = sb("den", [P, NH])
        rden = sb("rdenD", [P, NH])
        pT = sb("pT", [P, PAIRS, P])
        on = sb("on", [P, INNER])
        oT = sb("oT", [P, PAIRS, P])
        yc = sb("yc", [P, P])
        ysq = sb("ysq", [P, P])
        std = sb("stdD", [P, P])
        rstd = sb("rstdD", [P, P])
        yn0 = sb("yn0", [P, P])
        yn = sb("yn", [P, P])
        gate = sb("gate", [P, FFT, P])
        hid = sb("hid", [P, FFT, P])
        big = [ctx.enter_context(nc.psum_tensor(f"big{n}", [P, 2 * BANK], F32)) for n in range(3)]
        small = [ctx.enter_context(nc.psum_tensor(f"small{n}", [P, BANK], F32)) for n in range(2)]

        par, cst = sem("par"), sem("cst")
        w_qkv, w_o, w_ff, vmoved = sem("w_qkv"), sem("w_o"), sem("w_ff"), sem("vmoved")
        g_memset, v_memset, v_cst = sem("g_memset"), sem("v_memset"), sem("v_cst")
        (p_tq, p_tk, p_ot, p_q, p_mu, p_k, p_wo, p_v, p_var, p_pt, p_gate, p_a, p_s, p_pv, p_w2) = (
            sem(f"p_{n}") for n in ("tq", "tk", "otD", "q", "mu", "k", "wo", "vD", "var", "pt", "gate", "a", "s",
                                    "pvD", "w2"))
        (a_carry, a_qT, a_kT, a_oT, a_sqq, a_sqk, a_v, a_norm, a_std, a_pT, a_gelu, a_exp) = (
            sem(f"a_{n}") for n in ("carry", "qT", "kT", "oT", "sqq", "sqk", "vD", "norm", "stdD", "pT", "gelu", "expD"))
        (v_q, v_yc, v_ysq, v_ssq, v_k, v_ssk, v_clamp, v_rk, v_y, v_rstd, v_yn0, v_yn, v_hid, v_max, v_sub,
         v_on, v_den, v_rden, v_x) = (
            sem(f"v_{n}") for n in ("q", "yc", "ysq", "ssq", "k", "ssk", "clamp", "rk", "y", "rstdD", "yn0",
                                    "yn", "hid", "max", "sub", "on", "den", "rdenD", "x"))
        (g_addq, g_mulq, g_addk, g_mulk, g_xs, g_tab, g_ys) = (
            sem(f"g_{n}") for n in ("addq", "mulq", "addk", "mulk", "xs", "tab", "ys"))

        block = ctx.enter_context(nc.Block())
        NPAR, NQKV, NO, NFF, NVM = 15 * DEPTH, 5, 2, 5, 10

        def pipeline(eng, step):
            for i in range(LAST):
                step(i)
            with eng.Fori(LAST, STEPS) as i:
                step(i)
            for i in range(STEPS, STEPS + LAST):
                step(i)

        def on_tile(i, lag):
            n = i - lag
            return None if isinstance(n, int) and not 0 <= n < STEPS else n

        def upto(value):
            return min(value, STEPS) if isinstance(value, int) else value

        @block.sync
        def _(sp):
            def load_qkv(l):
                sp.wait_ge(v_memset, 4)
                for part in range(2):
                    src = lqkv[l, :, part * INNER:(part + 1) * INNER].rearrange("f (s p d) -> f s p d", s=2, d=HD)
                    dst = wqkv[:, part * INNER:(part + 1) * INNER].rearrange("f (p s d) -> f s p d", s=2, d=HD)
                    for s in range(2):
                        sp.dma_start(dst[:, s], src[:, s]).then_inc(w_qkv, 16)
                sp.dma_start(wqkv[:, 2 * INNER:], lqkv[l, :, 2 * INNER:]).then_inc(w_qkv, 16)

            def load_o(l):
                sp.wait_ge(v_memset, 4)
                src = lwo[l].rearrange("(s p d) n -> s d p n", s=2, d=HD)
                for s in range(2):
                    sp.dma_start(wo_sb[s * HD:(s + 1) * HD], src[s]).then_inc(w_o, 16)

            def load_ff(l):
                sp.wait_ge(v_memset, 4)
                for a in range(2):
                    sp.dma_start(w1_sb[:, a, 0:FF], lw1[l, :, a * FF:(a + 1) * FF]).then_inc(w_ff, 16)
                for j in range(FFT):
                    rows = P if j < FFT - 1 else FFL
                    sp.dma_start(w2_sb[0:rows, j, :], lw2[l, j * P:j * P + rows, :]).then_inc(w_ff, 16)

            def move_v(n, r, first=False):
                if first:
                    sp.wait_ge(a_v, n + 1)
                else:
                    sp.wait_ge(p_pv, n)
                sp.wait_ge(g_memset, 2)
                old = (r + 3) & 3
                cur, prev = vtile[:, r:r + 1, :], vtile[:, old:old + 1, :]
                for s in range(2):
                    half = slice(s * PAIRS * HD, (s + 1) * PAIRS * HD)
                    row = s * KEYS
                    dst = vwin[:].rearrange("p c s q d -> p c s (q d)")
                    sp.dma_start(dst[row:row + WIN, 0:1, s, :], prev[P - WIN:P, :, half]).then_inc(vmoved, 16)
                    sp.dma_start(dst[row + WIN:row + KEYS, 0:1, s, :], cur[0:WIN, :, half]).then_inc(vmoved, 16)
                    for c in range(1, NWIN):
                        sp.dma_start(dst[row:row + KEYS, c:c + 1, s, :],
                                     cur[WIN * (c - 1):WIN * (c + 1), :, half]).then_inc(vmoved, 16)

            load_qkv(0)
            load_o(0)
            load_ff(0)
            move_v(0, 0, first=True)
            for t in (1, 2):
                move_v(t, t)
            with sp.Fori(0, 3) as g:
                for t in range(3, 7):
                    move_v(g * 4 + t, t & 3)
            with sp.Fori(1, DEPTH) as l:
                sp.wait_ge(p_v, l * TILES)
                load_qkv(l)
                for t in range(-1, 2):
                    move_v(l * TILES + t, t & 3)
                sp.wait_ge(p_wo, l * TILES)
                load_o(l)
                move_v(l * TILES + 2, 2)
                sp.wait_ge(p_w2, l * TILES)
                load_ff(l)
                with sp.Fori(0, 3) as g:
                    for t in range(3, 7):
                        move_v(l * TILES + g * 4 + t, t & 3)
            move_v(STEPS - 1, 3)
            sp.wait_ge(vmoved, NVM * 16 * STEPS)

        @block.gpsimd
        def _(pool):
            pool.dma_start(rope_sb[:], rope).then_inc(cst, 16)
            pool.dma_start(cscale[:], carry_scale).then_inc(cst, 16)
            pool.dma_start(mask_f[:], mask).then_inc(cst, 16)
            pool.memset(vwin[:], 0.0).then_inc(g_memset, 1)
            pool.memset(vtile[:, 3, :], 0.0).then_inc(g_memset, 1)
            pool.memset(Y[:, 0:1], 0.0).then_inc(g_memset, 1)
            pool.wait_ge(cst, 48)
            pool.wait_ge(par, NPAR * 16)
            pool.wait_ge(v_memset, 4)

            def shift(dst, src, t, before, done, n):
                at = t * P
                pool.tensor_copy(dst[0:P // 2, :], src[0:P // 2, bass.ds(at + 1, P)])
                for s_before, value in before:
                    need(pool, s_before, value)
                pool.tensor_copy(dst[P // 2:P, :], src[P // 2:P, bass.ds(at, P)]).then_inc(done, 1)
                pool.wait_ge(done, n + 1)

            def prepare(n, before):
                t, l = n & (TILES - 1), layer_of(n)
                need(pool, p_v, n)
                shift(xs, X, t, before, g_xs, n)
                need(pool, v_k, n)
                src = rope_sb[:, bass.ds(t, 1), :, :].rearrange("p o k d -> p (o k) d")
                fac = scales[:, bass.ds(l, 1), :, :].rearrange("p o k d -> p (o k) d")
                pool.tensor_tensor(tab[:], src, fac, ALU.mult).then_inc(g_tab, 1)

            def step(i):
                if (n := on_tile(i, 0)) is not None:
                    for part, (done, add) in enumerate(((v_q, g_addq), (v_k, g_addk))):
                        pool.wait_ge(done, n + 1)
                        pool.tensor_tensor(rot[:, part], rot[:, part], rot2[:, part], ALU.add).then_inc(add, 1)
                    pool.wait_ge(v_rk, n + 1)
                    for part, (add, mul) in enumerate(((g_addq, g_mulq), (g_addk, g_mulk))):
                        pool.wait_ge(add, n + 1)
                        r3 = rot[:, part].rearrange("p (h d) -> p h d", d=HD)
                        pool.tensor_tensor(r3, r3, rnorm[:, part].unsqueeze(2).broadcast_to([P, NH, HD]),
                                           ALU.mult).then_inc(mul, 1)
                if (n := on_tile(i, 3)) is not None:
                    pool.wait_ge(v_y, n + 1)
                    need(pool, v_yc, n)
                    shift(ys, Y, n & (TILES - 1), [(g_mulk, upto(i + 1))], g_ys, n)
                if (n := on_tile(i, -1)) is not None:
                    prepare(n, [(g_mulk, n)])

            prepare(0, [(g_memset, 3)])
            for i in range(LAST):
                step(i)
            with pool.Fori(LAST, STEPS - 1) as i:
                step(i)
            for i in range(STEPS - 1, STEPS + LAST):
                step(i)

        @block.vector
        def _(dve):
            dve.memset(b1col[:], 0.0).then_inc(v_memset, 1)
            dve.memset(w1_sb[:], 0.0).then_inc(v_memset, 1)
            dve.memset(w2_sb[:], 0.0).then_inc(v_memset, 1)
            dve.memset(eps[:], EPS)
            dve.memset(kT[:], 0.0).then_inc(v_memset, 1)
            dve.memset(mean_w[:], 1.0 / DIM).then_inc(v_memset, 1)
            dve.wait_ge(cst, 48)
            dve.tensor_copy(mask_b[:], mask_f[:]).then_inc(v_cst, 1)
            dve.tensor_copy(ident_b[:], ident[:]).then_inc(v_cst, 1)
            dve.wait_ge(par, NPAR * 16)
            dve.wait_ge(g_memset, 3)

            def rotate(part, ps):
                x3 = ps[:].rearrange("p (h d) -> p h d", d=HD)
                r1 = rot[:, part].rearrange("p (h d) -> p h d", d=HD)
                r2 = rot2[:, part].rearrange("p (h d) -> p h d", d=HD)
                half = HD // 2
                dve.tensor_tensor(r1, x3, tab[:, 2 * part].unsqueeze(1).broadcast_to([P, NH, HD]), ALU.mult)
                for a, b in ((0, half), (half, 0)):
                    last = dve.tensor_tensor(r2[:, :, a:a + half], x3[:, :, b:b + half],
                                             tab[:, 2 * part + 1, a:a + half].unsqueeze(1)
                                             .broadcast_to([P, NH, half]), ALU.mult)
                return last

            def sum_squares(part, n, squares, s_sum):
                dve.wait_ge(squares, n + 1)
                dve.tensor_reduce(ssum[:, part], sq[:, part].rearrange("p (h d) -> p h d", d=HD), AX.X,
                                  ALU.add).then_inc(s_sum, 1)

            def step(i):
                if (n := on_tile(i, 0)) is not None:
                    dve.wait_ge(a_sqq, n + 1)
                    dve.wait_ge(g_tab, n + 1)
                    need(dve, p_tq, n)
                    need(dve, g_addq, n)
                    rotate(0, big[0]).then_inc(v_q, 1)
                if (n := on_tile(i, 4)) is not None:
                    dve.wait_ge(p_mu, n + 1)
                    dve.tensor_tensor(yc[:], small[0][:, 0:P], ys[:], ALU.subtract).then_inc(v_yc, 1)
                    dve.wait_ge(v_yc, n + 1)
                    need(dve, p_var, n)
                    dve.tensor_tensor(ysq[:], yc[:], yc[:], ALU.mult).then_inc(v_ysq, 1)
                if (n := on_tile(i, 0)) is not None:
                    sum_squares(0, n, a_sqq, v_ssq)
                    dve.wait_ge(a_sqk, n + 1)
                    need(dve, p_tk, n)
                    need(dve, g_addk, n)
                    rotate(1, big[1]).then_inc(v_k, 1)
                    sum_squares(1, n, a_sqk, v_ssk)
                    dve.wait_ge(v_ssk, n + 1)
                    need(dve, a_norm, n)
                    dve.tensor_scalar(clamped[:], ssum[:], 1e-24, None, ALU.max).then_inc(v_clamp, 1)
                if (n := on_tile(i, 3)) is not None:
                    dve.wait_ge(p_wo, n + 1)
                    cols = bass.ds((n & (TILES - 1)) * P + 1, P)
                    dve.tensor_tensor(Y[:, cols], small[1][:, 0:P], X[:, cols], ALU.add).then_inc(v_y, 1)
                if (n := on_tile(i, 0)) is not None:
                    dve.wait_ge(a_norm, n + 1)
                    need(dve, g_mulk, n)
                    dve.reciprocal(rnorm[:], norm[:]).then_inc(v_rk, 1)
                if (n := on_tile(i, 4)) is not None:
                    l = layer_of(n)
                    dve.wait_ge(a_std, n + 1)
                    dve.reciprocal(rstd[:], std[:]).then_inc(v_rstd, 1)
                    dve.wait_ge(v_rstd, n + 1)
                    dve.scalar_tensor_tensor(out=yn0[:], in0=yc[:], scalar=-1.0, in1=rstd[:], op0=ALU.mult,
                                             op1=ALU.mult).then_inc(v_yn0, 1)
                    dve.wait_ge(v_yn0, n + 1)
                    need(dve, p_a, n)
                    dve.tensor_scalar(yn[:], yn0[:], gcol[:, bass.ds(l, 1)], bcol[:, bass.ds(l, 1)], ALU.mult,
                                      ALU.add).then_inc(v_yn, 1)
                    dve.wait_ge(p_a, n + 1)
                    dve.wait_ge(a_gelu, n + 1)
                    need(dve, p_w2, n)
                    for j in range(FFT):
                        last = dve.scalar_tensor_tensor(
                            out=hid[:, j, :], in0=small[0][:, j * P:(j + 1) * P],
                            scalar=b1col[:, 0, j, bass.ds(l, 1)], in1=gate[:, j, :], op0=ALU.add, op1=ALU.mult)
                    last.then_inc(v_hid, 1)
                if (n := on_tile(i, 1)) is not None:
                    s3 = big[1][:].rearrange("p (h k) -> p h k", k=KEYS)
                    dve.wait_ge(p_s, n + 1)
                    dve.tensor_reduce(mx[:], s3, AX.X, ALU.max).then_inc(v_max, 1)
                    dve.wait_ge(v_max, n + 1)
                    need(dve, a_exp, n)
                    dve.tensor_tensor(shifted[:].rearrange("p (h k) -> p h k", k=KEYS), s3,
                                      mx[:].unsqueeze(2).broadcast_to([P, NH, KEYS]), ALU.subtract)\
                       .then_inc(v_sub, 1)
                if (n := on_tile(i, 2)) is not None:
                    dve.wait_ge(p_pv, n + 1)
                    dve.wait_ge(v_rden, n + 1)
                    need(dve, p_ot, n)
                    dve.tensor_tensor(on[:].rearrange("p (h d) -> p h d", d=HD),
                                      big[2][:].rearrange("p (h d) -> p h d", d=HD),
                                      rden[:].unsqueeze(2).broadcast_to([P, NH, HD]), ALU.mult).then_inc(v_on, 1)
                if (n := on_tile(i, 1)) is not None:
                    dve.wait_ge(a_exp, n + 1)
                    dve.tensor_reduce(den[:], prob[:].rearrange("p (h k) -> p h k", k=KEYS), AX.X,
                                      ALU.add).then_inc(v_den, 1)
                    dve.wait_ge(v_den, n + 1)
                    dve.reciprocal(rden[:], den[:]).then_inc(v_rden, 1)
                if (n := on_tile(i, 4)) is not None:
                    l = layer_of(n)
                    dve.wait_ge(p_w2, n + 1)
                    cols = bass.ds((n & (TILES - 1)) * P + 1, P)
                    dve.scalar_tensor_tensor(out=X[:, cols], in0=small[1][:, 0:P], scalar=b2col[:, bass.ds(l, 1)],
                                             in1=Y[:, cols], op0=ALU.add, op1=ALU.add).then_inc(v_x, 1)

            pipeline(dve, step)
            dve.wait_ge(v_x, STEPS)

        @block.scalar
        def _(act):
            for l in range(DEPTH):
                half = HD // 2
                for k, vec in ((0, lqs), (2, lks)):
                    row = vec[l].rearrange("(o d) -> o d", o=1)
                    act.dma_start(scales[:, l, k, :], row.broadcast_to([P, HD])).then_inc(par, 16)
                    for a, b in ((0, half), (half, 0)):
                        act.dma_start(scales[:, l, k + 1, a:a + half],
                                      row[:, b:b + half].broadcast_to([P, half])).then_inc(par, 16)
                for col, vec in ((gcol, lg), (bcol, lb), (b2col, lb2)):
                    act.dma_start(col[:, l:l + 1], vec[l].rearrange("(d o) -> d o", o=1)).then_inc(par, 16)
            act.wait_ge(v_memset, 4)
            for l in range(DEPTH):
                for a in range(2):
                    for j in range(FFT):
                        rows = P if j < FFT - 1 else FFL
                        src = lb1[l, a * FF + j * P:a * FF + j * P + rows].rearrange("(d o) -> d o", o=1)
                        act.dma_start(b1col[0:rows, a, j, l:l + 1], src).then_inc(par, 16)
            act.wait_ge(par, NPAR * 16)
            act.wait_ge(cst, 48)

            def copy(dst, src):
                return act.activation(dst, src, ACT.Copy)

            def step(i):
                if (n := on_tile(i, 1)) is not None:
                    need(act, p_s, n)
                    need(act, a_kT, n)
                    act.activation(kT[:, :, :, 0:WIN], kT[:, :, :, P:P + WIN], ACT.Copy,
                                   scale=cscale[:, 0:1]).then_inc(a_carry, 1)
                    act.wait_ge(p_tq, n + 1)
                    copy(qT[:].rearrange("p q t -> p (q t)"), big[0][:]).then_inc(a_qT, 1)
                    act.wait_ge(p_tk, n + 1)
                    act.wait_ge(a_carry, n + 1)
                    for s in range(2):
                        rows = slice(s * HD, (s + 1) * HD)
                        last = copy(kT[rows, :, s, WIN:WIN + P], big[1][rows].rearrange("p (q t) -> p q t", t=P))
                    last.then_inc(a_kT, 1)
                if (n := on_tile(i, 3)) is not None:
                    act.wait_ge(p_ot, n + 1)
                    need(act, p_wo, n)
                    copy(oT[:].rearrange("p q t -> p (q t)"), big[2][:]).then_inc(a_oT, 1)
                if (n := on_tile(i, 0)) is not None:
                    for part, ready, summed, done in ((0, p_q, v_ssq, a_sqq), (1, p_k, v_ssk, a_sqk)):
                        act.wait_ge(ready, n + 1)
                        need(act, summed, n)
                        act.activation(sq[:, part], big[part][:], ACT.Square).then_inc(done, 1)
                    act.wait_ge(p_v, n + 1)
                    need(act, vmoved, (n - 2) * (NVM * 16))
                    copy(vtile[:, bass.ds(n & 3, 1), :].rearrange("p o d -> p (o d)"), big[2][:]).then_inc(a_v, 1)
                    act.wait_ge(v_clamp, n + 1)
                    need(act, v_rk, n)
                    act.activation(norm[:], clamped[:], ACT.Sqrt).then_inc(a_norm, 1)
                if (n := on_tile(i, 4)) is not None:
                    act.wait_ge(p_var, n + 1)
                    need(act, v_rstd, n)
                    act.activation(std[:], small[0][:, 0:P], ACT.Sqrt, bias=eps[:, 0:1]).then_inc(a_std, 1)
                if (n := on_tile(i, 2)) is not None:
                    act.wait_ge(p_pt, n + 1)
                    need(act, p_pv, n)
                    copy(pT[:].rearrange("p q t -> p (q t)"), big[0][:]).then_inc(a_pT, 1)
                if (n := on_tile(i, 4)) is not None:
                    act.wait_ge(p_gate, n + 1)
                    need(act, v_hid, n)
                    for j in range(FFT):
                        last = act.activation(gate[:, j, :], small[1][:, j * P:(j + 1) * P], ACT.Gelu,
                                              bias=b1col[:, 1, j, bass.ds(layer_of(n), 1)])
                    last.then_inc(a_gelu, 1)
                if (n := on_tile(i, 1)) is not None:
                    act.wait_ge(v_sub, n + 1)
                    need(act, p_pt, n)
                    need(act, v_den, n)
                    act.activation(prob[:], shifted[:], ACT.Exp).then_inc(a_exp, 1)

            pipeline(act, step)

        @block.tensor
        def _(pe):
            pe.wait_ge(v_memset, 5)
            pe.wait_ge(v_cst, 2)

            def turn(ps, src):
                for p in range(PAIRS):
                    last = pe.transpose(ps[:, p * P:(p + 1) * P], src[:, p * P:(p + 1) * P], ident[:])
                return last

            def project(ps, part):
                for h in range(2):
                    at = part * INNER + h * BANK
                    last = pe.matmul(ps[:, h * BANK:(h + 1) * BANK], xs[:], wqkv[:, at:at + BANK],
                                     start=True, stop=True)
                return last

            def step(i):
                if (n := on_tile(i, 1)) is not None:
                    pe.wait_ge(g_mulq, n + 1)
                    need(pe, a_pT, upto(i - 2))
                    turn(big[0], rot[:, 0]).then_inc(p_tq, 1)
                    pe.wait_ge(g_mulk, n + 1)
                    need(pe, v_sub, i - 1)
                    turn(big[1], rot[:, 1]).then_inc(p_tk, 1)
                if (n := on_tile(i, 3)) is not None:
                    pe.wait_ge(v_on, n + 1)
                    turn(big[2], on).then_inc(p_ot, 1)
                if (n := on_tile(i, 0)) is not None:
                    pe.wait_ge(g_xs, n + 1)
                    pe.wait_ge(w_qkv, (layer_of(n) + 1) * (NQKV * 16))
                    need(pe, a_qT, i)
                    project(big[0], 0).then_inc(p_q, 1)
                if (n := on_tile(i, 4)) is not None:
                    pe.wait_ge(g_ys, n + 1)
                    need(pe, v_hid, n)
                    pe.matmul(small[0][:, 0:P], mean_w[:], ys[:], start=True, stop=True).then_inc(p_mu, 1)
                if (n := on_tile(i, 0)) is not None:
                    need(pe, a_kT, i)
                    project(big[1], 1).then_inc(p_k, 1)
                if (n := on_tile(i, 3)) is not None:
                    pe.wait_ge(a_oT, n + 1)
                    pe.wait_ge(w_o, (layer_of(n) + 1) * (NO * 16))
                    need(pe, v_x, n - 1)
                    for p in range(PAIRS):
                        last = pe.matmul(small[1][:, 0:P], wo_sb[:, p, :], oT[:, p, :],
                                         start=(p == 0), stop=(p == PAIRS - 1))
                    last.then_inc(p_wo, 1)
                if (n := on_tile(i, 0)) is not None:
                    need(pe, a_oT, i - 2)
                    project(big[2], 2).then_inc(p_v, 1)
                if (n := on_tile(i, 4)) is not None:
                    pe.wait_ge(v_ysq, n + 1)
                    pe.matmul(small[0][:, 0:P], mean_w[:], ysq[:], start=True, stop=True).then_inc(p_var, 1)
                if (n := on_tile(i, 2)) is not None:
                    pe.wait_ge(a_exp, n + 1)
                    pe.wait_ge(a_sqq, upto(i + 1))
                    pe.wait_ge(v_q, upto(i + 1))
                    need(pe, a_qT, upto(i))
                    turn(big[0], prob).then_inc(p_pt, 1)
                if (n := on_tile(i, 4)) is not None:
                    pe.wait_ge(v_yn, n + 1)
                    pe.wait_ge(w_ff, (layer_of(n) + 1) * (NFF * 16))
                    pe.wait_ge(a_std, n + 1)
                    need(pe, v_y, upto(i - 2))
                    for ps, a, done in ((small[1], 1, p_gate), (small[0], 0, p_a)):
                        for j in range(FFT):
                            last = pe.matmul(ps[:, j * P:(j + 1) * P], w1_sb[:, a, j * P:(j + 1) * P], yn[:],
                                             start=True, stop=True)
                        last.then_inc(done, 1)
                if (n := on_tile(i, 1)) is not None:
                    pe.wait_ge(a_qT, n + 1)
                    pe.wait_ge(a_kT, n + 1)
                    pe.wait_ge(a_sqk, upto(i + 1))
                    pe.wait_ge(v_k, upto(i + 1))
                    first = ((n & (TILES - 1)) + TILES - 1) >> 4
                    if not isinstance(n, int):
                        first = first.with_bounds(min_val=0, max_val=1)
                    m = mask_b[:, bass.ds(first, 1), :].broadcast_to([P, PAIRS, KEYS])
                    for h in range(2):
                        pe.matmul(big[1][:, h * BANK:(h + 1) * BANK].rearrange("p (h k) -> p h k", k=KEYS),
                                  ident_b[:], m, start=True, stop=False, skip_group_check=True)
                    for p in range(PAIRS):
                        for c in range(NWIN):
                            rows = slice(c * WIN, (c + 1) * WIN)
                            last = pe.matmul(big[1][rows, p * P:(p + 1) * P], qT[:, p, rows],
                                             kT[:, p, :, c * WIN:c * WIN + KEYS], start=False, stop=True,
                                             skip_group_check=True)
                    last.then_inc(p_s, 1)
                if (n := on_tile(i, 2)) is not None:
                    pe.wait_ge(a_pT, n + 1)
                    pe.wait_ge(vmoved, (n + 1) * (NVM * 16))
                    pe.wait_ge(a_v, upto(i + 1))
                    need(pe, a_oT, upto(i - 2))
                    for p in range(PAIRS):
                        for c in range(NWIN):
                            rows = slice(c * WIN, (c + 1) * WIN)
                            last = pe.matmul(big[2][rows, p * P:(p + 1) * P], pT[:, p, rows], vwin[:, c, :, p, :],
                                             start=True, stop=True, skip_group_check=True)
                    last.then_inc(p_pv, 1)
                if (n := on_tile(i, 4)) is not None:
                    pe.wait_ge(v_hid, n + 1)
                    for j in range(FFT):
                        last = pe.matmul(small[1][:, 0:P], w2_sb[:, j, :], hid[:, j, :],
                                         start=(j == 0), stop=(j == FFT - 1))
                    last.then_inc(p_w2, 1)

            pipeline(pe, step)


def stage_e(nc, x, ident, X, att, out):
    with ExitStack() as ctx:
        def sem(name):
            return ctx.enter_context(nc.semaphore(name))

        xin = ctx.enter_context(nc.sbuf_tensor("xinE", [P, TILES, DIM], F32))
        g = ctx.enter_context(nc.sbuf_tensor("gE", [P, SEQ], F32))
        z = ctx.enter_context(nc.sbuf_tensor("zE", [P, SEQ], F32))
        res = ctx.enter_context(nc.sbuf_tensor("resE", [P, TILES, DIM], F32))
        ps = ctx.enter_context(nc.psum_tensor("psE", [P, 4, BANK], F32))
        x_in, stored, a_g, v_z, p_z, v_res = (sem(n) for n in ("x_inE", "storedE", "a_g", "v_z", "p_z", "v_res"))
        block = ctx.enter_context(nc.Block())

        @block.sync
        def _(sp):
            sp.dma_start(xin[:], x[0].rearrange("(t p) d -> p t d", p=P)).then_inc(x_in, 16)
            rows = out[0].rearrange("(t p) d -> p t d", p=P)
            for c in range(4):
                sp.wait_ge(v_res, c + 1)
                sp.dma_start(rows[:, 4 * c:4 * c + 4], res[:, 4 * c:4 * c + 4]).then_inc(stored, 16)
            sp.wait_ge(stored, 64)

        @block.scalar
        def _(act):
            for c in range(4):
                act.activation(g[:, c * BANK:(c + 1) * BANK], X[:, 1 + c * BANK:1 + (c + 1) * BANK],
                               ACT.Silu).then_inc(a_g, 1)

        @block.vector
        def _(dve):
            dve.wait_ge(x_in, 16)
            for c in range(4):
                cols = slice(c * BANK, (c + 1) * BANK)
                dve.wait_ge(a_g, c + 1)
                dve.tensor_tensor(z[:, cols], att[:, cols], g[:, cols], ALU.mult).then_inc(v_z, 1)
            for c in range(4):
                dve.wait_ge(p_z, c + 1)
                dve.tensor_tensor(res[:, 4 * c:4 * c + 4], ps[:, c, :].rearrange("p (t d) -> p t d", t=4),
                                  xin[:, 4 * c:4 * c + 4], ALU.add).then_inc(v_res, 1)

        @block.tensor
        def _(pe):
            for t in range(TILES):
                if t % 4 == 0:
                    pe.wait_ge(v_z, t // 4 + 1)
                last = pe.transpose(ps[:, t // 4, t % 4 * P:(t % 4 + 1) * P], z[:, t * P:(t + 1) * P], ident[:])
                if t % 4 == 3:
                    last.then_inc(p_z, 1)


def shape_tables():
    f = np.float32
    half = np.arange(0, HD, 2, dtype=f)
    inv_freq = (f(1) / f(10000) ** (half / f(HD))).astype(f)
    angle = np.arange(SEQ, dtype=f)[:, None] * inv_freq[None, :]
    angle = np.concatenate([angle, angle], -1).astype(np.float64)
    base = ((half + 0.4 * HD) / (1.4 * HD)).astype(f).astype(np.float64)
    base = np.concatenate([base, base])
    power = (np.arange(SEQ) % P - P // 2) / (WIN // 2)
    scale = base[None, :] ** power[:, None]
    sign = np.where(np.arange(HD) < HD // 2, -1.0, 1.0)
    cos, sin = np.cos(angle), np.sin(angle) * sign
    rope = np.stack([8.0 * cos * scale, 8.0 * sin * scale, cos / scale, sin / scale], 1)
    rope = rope.reshape(TILES, P, 4, HD).transpose(1, 0, 2, 3).astype(f)
    carry = np.tile(base ** (P / (WIN // 2)), 2).reshape(P, 1).astype(f)
    row, key = np.arange(P)[:, None] % WIN, np.arange(KEYS)[None, :]
    ok = (row <= key) & (key <= row + WIN)
    first = ok & ((np.arange(P)[:, None] >= WIN) | (key >= WIN))
    mask = np.where(np.stack([first, ok], 1), 0.0, -1e30).astype(f)
    return {"rope": np.ascontiguousarray(rope), "carry_scale": carry, "mask": mask, "eye": np.eye(P, dtype=f)}


_INS = ["L0_attn_x", "L0_attn_Wv", "L0_attn_Wk", "L0_attn_Wq", "L0_attn_Wo", "L0_attn_bo", "L0_ffn_Wqkv",
        "L0_ffn_q_scale", "L0_ffn_k_scale", "L0_ffn_Wo", "L0_ffn_ln_g", "L0_ffn_ln_b", "L0_ffn_W1", "L0_ffn_b1",
        "L0_ffn_W2", "L0_ffn_b2"]


def kernel(**inputs):
    import concourse.bacc as _bacc
    from concourse.bass_utils import run_bass_kernel_spmd as _run

    nc = _bacc.Bacc("TRN2", target_bir_lowering=False, num_devices=1)
    arrays, args = {}, []
    tables = shape_tables()
    for name in _INS + list(tables):
        a = np.ascontiguousarray(tables[name] if name in tables else inputs[name])
        arrays[f"in_{name}"] = a
        args.append(nc.dram_tensor(f"in_{name}", a.shape, mybir.dt.from_np(a.dtype), kind="ExternalInput").ap())
    out = nc.dram_tensor("out_0", (1, SEQ, DIM), F32, kind="ExternalOutput").ap()
    build(nc, *args, out)
    r = _run(nc, [arrays], core_ids=[0])
    return r.results[0]["out_0"]
```

```python
from contextlib import ExitStack

import numpy as np

import concourse.bass as bass
from concourse import mybir

F32 = mybir.dt.float32
F32R = mybir.dt.float32r
BF16 = mybir.dt.bfloat16
ALU = mybir.AluOpType
ACT = mybir.ActivationFunctionType
AX = mybir.AxisListType

P = 128
SEQ = 2048
DIM = 128
TILES = SEQ // P
BANK = 512

GH = 16
GD = DIM // GH
SPLIT = 4 * GD
GBUF = 4
MAXSTEP = 13
RING = 3
ROUND = 4 * (4 * TILES + 2)
LEAD = 20
PSLOTS = 8
PVLAG = 2
VCOL = 32

DEPTH = 6
NH = 16
HD = 64
PAIRS = NH // 2
WIN = 32
NWIN = P // WIN
KEYS = 2 * WIN
INNER = NH * HD
FF = int(DIM * 4 * 2 / 3)
FFT = 3
FFL = FF - (FFT - 1) * P
STEPS = DEPTH * TILES
EPS = 1e-5
LAST = 5


def need(eng, sem, value):
    if not isinstance(value, int) or value > 0:
        eng.wait_ge(sem, value)


def layer_of(n):
    l = n // TILES if isinstance(n, int) else (n >> 4)
    return l if isinstance(n, int) else l.with_bounds(min_val=0, max_val=DEPTH - 1)


def build(nc, x, wv, wk, wq, wo, bo, lqkv, lqs, lks, lwo, lg, lb, lw1, lb1, lw2, lb2,
          rope, carry_scale, mask, eye, out):
    scratch = nc.dram_tensor("split_operands", [4, DIM, SEQ], F32, kind="Internal").ap()
    max_scratch = nc.dram_tensor("maxima", [2, TILES, P], F32, kind="Internal").ap()
    persistent = ExitStack()

    def keep(name, shape, dt=F32):
        return persistent.enter_context(nc.sbuf_tensor(name, shape, dt))

    with persistent:
        ident = keep("ident", [P, P])
        X = keep("X", [P, 1 + SEQ])
        att = keep("att", [P, SEQ])
        with ExitStack() as ctx:
            vtok = ctx.enter_context(nc.sbuf_tensor("vtok", [P, TILES, DIM], F32))
            otok = ctx.enter_context(nc.sbuf_tensor("otok", [P, TILES, DIM], F32))
            wout = ctx.enter_context(nc.sbuf_tensor("wout", [P, DIM], F32))
            bout = ctx.enter_context(nc.sbuf_tensor("bout", [P, 1], F32))
            stage_a(nc, x, wq, wk, wv, wo, bo, eye, scratch, ident, X, vtok, wout, bout)
            stage_b(nc, scratch, max_scratch, ident, vtok, otok)
            stage_c(nc, ident, otok, wout, bout, att)
        stage_d(nc, lqkv, lqs, lks, lwo, lg, lb, lw1, lb1, lw2, lb2, rope, carry_scale, mask, ident, X)
        stage_e(nc, x, ident, X, att, out)


def stage_a(nc, x, wq, wk, wv, wo, bo, eye, scratch, ident, X, vtok, wout, bout):
    with ExitStack() as ctx:
        def sb(name, shape, dt=F32):
            return ctx.enter_context(nc.sbuf_tensor(name, shape, dt))

        def sem(name):
            return ctx.enter_context(nc.semaphore(name))

        xin = sb("xin", [P, TILES, DIM])
        xc = sb("xc", [P, TILES, DIM])
        sq = sb("sq", [P, TILES, DIM])
        mean = sb("mean", [P, TILES])
        std = sb("std", [P, TILES])
        rstd = sb("rstd", [P, TILES])
        w = sb("w_in", [P, 3, DIM])
        split = sb("split", [P, 4, SEQ], F32R)
        ps = ctx.enter_context(nc.psum_tensor("psA", [P, 8, BANK], F32))

        x_in, w_in, cst_in, stored = sem("x_in"), sem("w_in_s"), sem("cst_in"), sem("stored")
        v_sum, v_mean, v_xc, v_var, v_rstd, v_xn = (sem(f"v_{n}") for n in ("sum", "mean", "xc", "var", "rstd", "xn"))
        a_sq, p_xt, a_xt, p_qk, v_hi, v_lo, p_v, a_v = (
            sem(n) for n in ("a_sq", "p_xt", "a_xt", "p_qk", "v_hi", "v_lo", "p_v", "a_v"))
        g_zero, a_std = sem("g_zero"), sem("a_std")

        block = ctx.enter_context(nc.Block())

        @block.sync
        def _(sp):
            sp.dma_start(xin[:], x[0].rearrange("(t p) d -> p t d", p=P)).then_inc(x_in, 16)
            sp.dma_start(ident[:], eye).then_inc(cst_in, 16)
            for n, src in enumerate((wq, wk, wv)):
                sp.dma_start(w[:, n, :], src).then_inc(w_in, 16)
            sp.dma_start(wout[:], wo).then_inc(cst_in, 16)
            sp.dma_start(bout[:], bo.rearrange("(d a) -> d a", a=1)).then_inc(cst_in, 16)
            for n in range(4):
                sp.wait_ge(v_hi if n % 2 == 0 else v_lo, 4 * (n // 2 + 1))
                sp.dma_start(scratch[n], split[:, n, :].bitcast(F32)).then_inc(stored, 16)
            sp.wait_ge(stored, 64)

        @block.gpsimd
        def _(pool):
            pool.memset(X[:, 0:1], 0.0).then_inc(g_zero, 1)

        @block.vector
        def _(dve):
            dve.wait_ge(x_in, 16)
            dve.tensor_reduce(mean[:], xin[:], AX.X, ALU.add).then_inc(v_sum, 1)
            dve.wait_ge(v_sum, 1)
            dve.tensor_scalar(mean[:], mean[:], 1.0 / DIM, None, ALU.mult).then_inc(v_mean, 1)
            dve.wait_ge(v_mean, 1)
            dve.tensor_tensor(xc[:], xin[:], mean[:].unsqueeze(2).broadcast_to([P, TILES, DIM]),
                              ALU.subtract).then_inc(v_xc, 1)
            dve.wait_ge(a_sq, 1)
            dve.tensor_reduce(rstd[:], sq[:], AX.X, ALU.add).then_inc(v_var, 1)
            dve.wait_ge(v_var, 1)
            dve.tensor_scalar(rstd[:], rstd[:], 1.0 / DIM, EPS, ALU.mult, ALU.add).then_inc(v_rstd, 1)
            dve.wait_ge(a_std, 1)
            dve.reciprocal(rstd[:], std[:]).then_inc(v_rstd, 1)
            dve.wait_ge(v_rstd, 2)
            dve.tensor_tensor(xc[:], xc[:], rstd[:].unsqueeze(2).broadcast_to([P, TILES, DIM]),
                              ALU.mult).then_inc(v_xn, 1)
            for m in range(8):
                n, c = m // 4, m % 4
                dve.wait_ge(p_qk, m + 1)
                hi, lo = split[:, 2 * n, c * BANK:(c + 1) * BANK], split[:, 2 * n + 1, c * BANK:(c + 1) * BANK]
                dve.tensor_copy(hi, ps[:, m, :]).then_inc(v_hi, 1)
                dve.wait_ge(v_hi, m + 1)
                dve.tensor_tensor(lo, ps[:, m, :], hi.bitcast(F32), ALU.subtract).then_inc(v_lo, 1)

        @block.scalar
        def _(act):
            act.wait_ge(v_xc, 1)
            act.activation(sq[:], xc[:], ACT.Square).then_inc(a_sq, 1)
            act.wait_ge(v_rstd, 1)
            act.activation(std[:], rstd[:], ACT.Sqrt).then_inc(a_std, 1)
            for c in range(4):
                act.wait_ge(p_xt, c + 1)
                act.activation(X[:, 1 + c * BANK:1 + (c + 1) * BANK], ps[:, c, :], ACT.Copy).then_inc(a_xt, 1)
            for c in range(4):
                act.wait_ge(p_v, c + 1)
                act.activation(vtok[:, 4 * c:4 * c + 4, :], ps[:, c, :].rearrange("p (t d) -> p t d", t=4),
                               ACT.Copy).then_inc(a_v, 1)

        @block.tensor
        def _(pe):
            pe.wait_ge(cst_in, 48)
            pe.wait_ge(v_xn, 1)
            for t in range(TILES):
                last = pe.transpose(ps[:, t // 4, t % 4 * P:(t % 4 + 1) * P], xc[:, t, :], ident[:])
                if t % 4 == 3:
                    last.then_inc(p_xt, 1)
            pe.wait_ge(w_in, 48)
            pe.wait_ge(a_xt, 4)
            for m in range(8):
                n, c = m // 4, m % 4
                pe.matmul(ps[:, m, :], w[:, n, :], X[:, 1 + c * BANK:1 + (c + 1) * BANK],
                          start=True, stop=True).then_inc(p_qk, 1)
            for t in range(TILES):
                if t % 4 == 0:
                    pe.wait_ge(v_lo, t // 4 + 1)
                last = pe.matmul(ps[:, t // 4, t % 4 * P:(t % 4 + 1) * P], X[:, 1 + t * P:1 + (t + 1) * P],
                                 w[:, 2, :], start=True, stop=True)
                if t % 4 == 3:
                    last.then_inc(p_v, 1)


def ring_slots():
    slots, n = {}, 0
    for w in range(-LEAD, GH * TILES):
        if w + LEAD < GH * TILES:
            for c in range(4):
                slots["scores", w + LEAD, c] = n
                n += 1
        h = w // TILES
        if h >= 1 and w % TILES == PVLAG:
            slots["output", h - 1] = n
            n += 1
        if -1 <= h < GH - 1 and w % TILES == MAXSTEP:
            slots["maxima", h + 1] = n
            n += 1
    slots["output", GH - 1] = n
    return slots


def stage_b(nc, scratch, max_scratch, ident, vtok, otok):
    WARM = 20
    TOTAL = GH * TILES
    with ExitStack() as ctx:
        def sb(name, shape, dt=F32):
            return ctx.enter_context(nc.sbuf_tensor(name, shape, dt))

        def pb(name, shape):
            return ctx.enter_context(nc.psum_tensor(name, shape, F32))

        def sem(name):
            return ctx.enter_context(nc.semaphore(name))

        qs = sb("qs", [P, GBUF, SEQ], F32R)
        ks = sb("ks", [P, GBUF, SEQ], F32R)
        zero2 = sb("zero2", [2, SEQ], F32R)
        vs = sb("vs", [P, 2, TILES, VCOL])
        prob = sb("prob", [P, PSLOTS, SEQ])
        part = sb("part", [P, 2, TILES, 4])
        nmax = sb("nmax", [P, TILES])
        nmax_hi = sb("nmax_hi", [TILES, P], F32R)
        nmax_lo = sb("nmax_lo", [TILES, P], F32R)
        oacc = sb("oacc", [P, BANK])
        rden = sb("rden", [P, 4, 4])
        ps_ring = pb("ps_ring", [P, RING, BANK])
        ps_exp = pb("ps_exp", [P, 2, 2 * BANK])
        ps_o = pb("ps_o", [P, BANK])

        loaded = [sem(f"loaded{b}") for b in range(GBUF)]
        max_out, max_rows = sem("max_out"), sem("max_rows")
        g_init, v_init, g_vs = sem("g_init"), sem("v_init"), sem("g_vs")
        p_max, v_ring, v_nmax, p_maxt, v_mhi = (
            sem(n) for n in ("p_max", "v_ring", "v_nmax", "p_maxt", "v_mhi"))
        p_exp, a_exp, p_pv, a_oacc, p_ot, v_rden = (
            sem(n) for n in ("p_exp", "a_exp", "p_pv", "a_oacc", "p_otr", "v_rdenB"))
        slots = ring_slots()
        LOADS = 9

        block = ctx.enter_context(nc.Block())

        def walk(eng, step):
            for w in range(WARM):
                step(w, w, 0)
            with eng.Fori(0, 3) as g:
                for k in range(WARM, WARM + 4 * TILES):
                    step(g * (4 * TILES) + k, k, g)
            for w in range(WARM + 12 * TILES, TOTAL):
                step(w, w, 0)

        @block.sync
        def _(sp):
            def load(h, b):
                rows = bass.ds(h * GD, GD)
                for r, (qn, kn) in enumerate(((0, 2), (0, 3), (1, 2), (1, 3))):
                    sp.dma_start(qs[r * GD:(r + 1) * GD, b, :].bitcast(F32), scratch[qn, rows, :]).then_inc(loaded[b], 16)
                    sp.dma_start(ks[r * GD:(r + 1) * GD, b, :].bitcast(F32), scratch[kn, rows, :]).then_inc(loaded[b], 16)
                sp.dma_start(qs[SPLIT:SPLIT + 2, b, :].bitcast(F32), zero2[:].bitcast(F32)).then_inc(loaded[b], 16)

            def put_max(h, b, used):
                sp.wait_ge(v_ring, used)
                for r, src in ((0, nmax_hi), (1, nmax_lo)):
                    sp.dma_start(max_scratch[r], src[:].bitcast(F32)).then_inc(max_out, 16)
                sp.wait_ge(max_out, h * 32 + 32)
                sp.dma_start(qs[SPLIT:SPLIT + 2, b, :].bitcast(F32),
                             max_scratch.rearrange("r t q -> r (t q)")).then_inc(max_rows, 16)

            sp.wait_ge(g_init, 3)
            sp.wait_ge(v_init, 4)
            for h in range(GBUF):
                load(h, h)
            put_max(0, 0, slots["maxima", 0] + 1)

            def head(h, k, lead):
                put_max(h, k % GBUF, lead * ROUND + (slots["maxima", k] + 1))
                sp.wait_ge(p_exp, 2 * TILES * h)
                sp.wait_ge(p_pv, TILES * (h - 1) + 1) if k > 1 else None
                load(h + GBUF - 1, (k - 1) % GBUF)

            with sp.Fori(0, 3) as g:
                for k in range(1, 5):
                    head(g * 4 + k, k, g)
            for h in range(13, GH):
                put_max(h, h % GBUF, slots["maxima", h] + 1)
            sp.wait_ge(max_rows, 16 * GH)

        @block.gpsimd
        def _(pool):
            pool.memset(zero2[:].bitcast(F32), 0.0).then_inc(g_init, 1)
            pool.memset(vs[:], 0.0).then_inc(g_init, 1)
            pool.wait_ge(g_init, 2)
            pool.memset(vs[:, :, :, GD:GD + 1], 1.0).then_inc(g_init, 1)
            pool.wait_ge(g_init, 3)

            def values(h, b):
                pool.tensor_copy(vs[:, b, :, 0:GD], vtok[:, :, bass.ds(h * GD, GD)]).then_inc(g_vs, 1)

            values(0, 0)
            values(1, 1)
            with pool.Fori(1, GH // 2) as hh:
                for b in range(2):
                    pool.wait_ge(p_pv, TILES * (hh * 2 + b - 1))
                    values(hh * 2 + b, b)

        @block.vector
        def _(dve):
            for b in range(GBUF):
                dve.memset(qs[:, b, :].bitcast(F32), 0.0)
                dve.memset(ks[:, b, :].bitcast(F32), 0.0).then_inc(v_init, 1)
            dve.wait_ge(v_init, 4)
            dve.memset(ks[SPLIT:SPLIT + 2, :, :].bitcast(F32), 1.0).then_inc(v_init, 1)

            def reduce_tile(u, ku, lead):
                t, b = ku % TILES, ku // TILES % 2
                for c in range(4):
                    dve.wait_ge(p_max, u * 4 + c + 1)
                    dve.tensor_reduce(part[:, b, t, c:c + 1], ps_ring[:, slots["scores", ku, c] % RING, :], AX.X,
                                      ALU.max).then_inc(v_ring, 1)
                if t == TILES - 1:
                    dve.wait_ge(v_ring, lead * ROUND + (slots["scores", ku, 3] + 1))
                    if ku >= TILES:
                        dve.wait_ge(p_maxt, (u - (TILES - 1)) // TILES)
                    dve.tensor_reduce(nmax[:], part[:, b], AX.X, ALU.max, negate=True).then_inc(v_nmax, 1)

            def split_max(h, kh):
                src = ps_ring[0:TILES, slots["maxima", kh] % RING, 0:P]
                dve.wait_ge(p_maxt, h + 1)
                if kh > 0:
                    dve.wait_ge(max_rows, h * 16)
                dve.tensor_copy(nmax_hi[:], src).then_inc(v_mhi, 1)
                dve.wait_ge(v_mhi, h + 1)
                dve.tensor_tensor(nmax_lo[:], src, nmax_hi[:].bitcast(F32), ALU.subtract).then_inc(v_ring, 1)

            def finish_head(h, kh):
                dve.wait_ge(p_ot, h + 1)
                if kh == GH - 1:
                    dve.wait_ge(v_ring, slots["output", kh])
                o = ps_ring[:, slots["output", kh] % RING, :].rearrange("p (s c m) -> p c s m", s=4, c=4)
                dve.reciprocal(rden[:], o[:, :, :, GD]).then_inc(v_rden, 1)
                dve.wait_ge(v_rden, h + 1)
                dve.tensor_tensor(otok[:, :, bass.ds(h * GD, GD)].rearrange("p (c s) d -> p c s d", c=4),
                                  o[:, :, :, 0:GD], rden[:].unsqueeze(3).broadcast_to([P, 4, 4, GD]),
                                  ALU.mult).then_inc(v_ring, 1)

            for u in range(LEAD):
                reduce_tile(u, u, 0)
                if u - LEAD == MAXSTEP - TILES:
                    split_max(0, 0)

            def step(w, k, lead):
                if not (isinstance(w, int) and w + LEAD >= TOTAL):
                    reduce_tile(w + LEAD, k + LEAD, lead)
                if k % TILES == PVLAG and k > PVLAG:
                    finish_head(lead * 4 + (k // TILES - 1), k // TILES - 1)
                if k % TILES == MAXSTEP and k < TOTAL - TILES:
                    split_max(lead * 4 + (k // TILES + 1), k // TILES + 1)

            walk(dve, step)
            finish_head(GH - 1, GH - 1)

        @block.scalar
        def _(act):
            def step(w, k, lead):
                for half in range(2):
                    act.wait_ge(p_exp, w * 2 + half + 1)
                    if k >= PSLOTS:
                        act.wait_ge(p_pv, lead * (4 * TILES) + (k - PSLOTS + 1))
                    act.activation(prob[:, k % PSLOTS, half * 2 * BANK:(half + 1) * 2 * BANK],
                                   ps_exp[:, half, :], ACT.Exp, scale=GD ** -0.5).then_inc(a_exp, 1)
                if k % TILES == 1 and k > 1:
                    save_o(lead * 4 + (k // TILES - 1), k > TILES + 1)

            def save_o(h, later):
                act.wait_ge(p_pv, (h + 1) * TILES)
                if later:
                    act.wait_ge(p_ot, h)
                act.activation(oacc[:], ps_o[:], ACT.Copy).then_inc(a_oacc, 1)

            walk(act, step)
            save_o(GH - 1, True)

        @block.tensor
        def _(pe):
            pe.wait_ge(v_init, 5)

            def free_slot(n, lead):
                if n >= RING:
                    pe.wait_ge(v_ring, lead * ROUND + (n - RING + 1))
                return n % RING

            def max_scores(u, ku, c, lead):
                b, t = ku // TILES % GBUF, ku % TILES
                if t == 0 and c == 0:
                    pe.wait_ge(loaded[b], ((u - ku % (GBUF * TILES)) // (GBUF * TILES) + 1) * (LOADS * 16))
                r = free_slot(slots["scores", ku, c], lead)
                pe.matmul(ps_ring[:, r, :], qs[:, b, t * P:(t + 1) * P], ks[:, b, c * BANK:(c + 1) * BANK],
                          start=True, stop=True).then_inc(p_max, 1)

            def turn_max(h, kh, lead):
                pe.wait_ge(v_nmax, h + 1)
                r = free_slot(slots["maxima", kh], lead)
                pe.transpose(ps_ring[0:TILES, r, 0:P], nmax[:], ident[:]).then_inc(p_maxt, 1)

            def turn_o(h, kh, lead):
                pe.wait_ge(a_oacc, h + 1)
                r = free_slot(slots["output", kh], lead)
                for s in range(4):
                    last = pe.transpose(ps_ring[:, r, s * P:(s + 1) * P], oacc[:, s * P:(s + 1) * P], ident[:])
                last.then_inc(p_ot, 1)

            def exp_scores(w, k, half):
                b, t = k // TILES % GBUF, k % TILES
                if t == 0 and half == 0:
                    pe.wait_ge(max_rows, (w // TILES + 1) * 16)
                if k > 0:
                    pe.wait_ge(a_exp, w * 2 + half - 1)
                for cc in range(2):
                    last = pe.matmul(ps_exp[:, half, cc * BANK:(cc + 1) * BANK], ks[:, b, t * P:(t + 1) * P],
                                     qs[:, b, (2 * half + cc) * BANK:(2 * half + cc + 1) * BANK],
                                     start=True, stop=True)
                last.then_inc(p_exp, 1)

            def value_products(w, k):
                kk = k - PVLAG
                h, t = kk // TILES, kk % TILES
                if t == 0:
                    pe.wait_ge(g_vs, (w - PVLAG) // TILES + 1)
                    if kk >= TILES:
                        pe.wait_ge(a_oacc, (w - PVLAG) // TILES)
                pe.wait_ge(a_exp, (w - PVLAG) * 2 + 2)
                for c in range(4):
                    last = pe.matmul(ps_o[32 * c:32 * c + VCOL, :], vs[:, h % 2, t, :],
                                     prob[:, kk % PSLOTS, c * BANK:(c + 1) * BANK],
                                     start=(t == 0), stop=(t == TILES - 1), skip_group_check=True)
                last.then_inc(p_pv, 1)

            for u in range(LEAD):
                for c in range(4):
                    max_scores(u, u, c, 0)
                if u - LEAD == MAXSTEP - TILES:
                    turn_max(0, 0, 0)

            def step(w, k, lead):
                ahead = not (isinstance(w, int) and w + LEAD >= TOTAL)
                if ahead:
                    max_scores(w + LEAD, k + LEAD, 0, lead)
                    max_scores(w + LEAD, k + LEAD, 1, lead)
                exp_scores(w, k, 0)
                exp_scores(w, k, 1)
                if ahead:
                    max_scores(w + LEAD, k + LEAD, 2, lead)
                    max_scores(w + LEAD, k + LEAD, 3, lead)
                if k >= PVLAG:
                    value_products(w, k)
                if k % TILES == PVLAG and k > PVLAG:
                    turn_o(lead * 4 + (k // TILES - 1), k // TILES - 1, lead)
                if k % TILES == MAXSTEP and k < TOTAL - TILES:
                    turn_max(lead * 4 + (k // TILES + 1), k // TILES + 1, lead)

            walk(pe, step)
            for w in range(TOTAL, TOTAL + PVLAG):
                value_products(w, w)
            turn_o(GH - 1, GH - 1, 0)


def stage_c(nc, ident, otok, wout, bout, att):
    with ExitStack() as ctx:
        def sem(name):
            return ctx.enter_context(nc.semaphore(name))

        ot = ctx.enter_context(nc.sbuf_tensor("ot", [P, SEQ], F32))
        ps = ctx.enter_context(nc.psum_tensor("psC", [P, 8, BANK], F32))
        p_t, a_t, p_w, v_w = sem("p_t"), sem("a_t"), sem("p_w"), sem("v_w")
        block = ctx.enter_context(nc.Block())

        @block.tensor
        def _(pe):
            for t in range(TILES):
                last = pe.transpose(ps[:, t // 4, t % 4 * P:(t % 4 + 1) * P], otok[:, t, :], ident[:])
                if t % 4 == 3:
                    last.then_inc(p_t, 1)
            for c in range(4):
                pe.wait_ge(a_t, c + 1)
                pe.matmul(ps[:, 4 + c, :], wout[:], ot[:, c * BANK:(c + 1) * BANK],
                          start=True, stop=True).then_inc(p_w, 1)

        @block.scalar
        def _(act):
            for c in range(4):
                act.wait_ge(p_t, c + 1)
                act.activation(ot[:, c * BANK:(c + 1) * BANK], ps[:, c, :], ACT.Copy).then_inc(a_t, 1)

        @block.vector
        def _(dve):
            for c in range(4):
                dve.wait_ge(p_w, c + 1)
                dve.tensor_scalar(att[:, c * BANK:(c + 1) * BANK], ps[:, 4 + c, :], bout[:, 0:1], None,
                                  ALU.add).then_inc(v_w, 1)
            dve.wait_ge(v_w, 4)


def stage_d(nc, lqkv, lqs, lks, lwo, lg, lb, lw1, lb1, lw2, lb2, rope, carry_scale, mask, ident, X):
    with ExitStack() as ctx:
        def sb(name, shape, dt=F32):
            return ctx.enter_context(nc.sbuf_tensor(name, shape, dt))

        def sem(name):
            return ctx.enter_context(nc.semaphore(name))

        wqkv = sb("wqkv", [P, 2, 3 * INNER])
        wo_sb = sb("wo_sb", [P, PAIRS, DIM])
        w1_sb = sb("w1_sb", [P, 2, FFT * P])
        w2_sb = sb("w2_sb", [P, FFT, DIM])
        scales = sb("scales", [P, DEPTH, 4, HD])
        gcol = sb("gcol", [P, DEPTH])
        bcol = sb("bcol", [P, DEPTH])
        b2col = sb("b2col", [P, DEPTH])
        b1col = sb("b1col", [P, 2, FFT, DEPTH])
        rope_sb = sb("rope_sb", [P, TILES, 4, HD])
        cscale = sb("cscale", [P, 1])
        mask_f = sb("mask_f", [P, 2, KEYS])
        mask_b = sb("mask_b", [P, 2, KEYS], BF16)
        ident_b = sb("ident_b", [P, P], BF16)
        mean_w = sb("mean_w", [P, P])
        eps = sb("eps", [P, 1])
        Y = sb("Y", [P, 1 + SEQ])
        xs = sb("xs", [P, P])
        ys = sb("ys", [P, P])
        tab = sb("tab", [P, 4, HD])
        rot = sb("rot", [P, 2, INNER])
        rot2 = sb("rot2", [P, 2, INNER])
        rotn = sb("rotn", [P, 2, INNER])
        sq = sb("sqD", [P, 2, INNER])
        ssum = sb("ssum", [P, 2, NH])
        clamped = sb("clamped", [P, 2, NH])
        norm = sb("norm", [P, 2, NH])
        rnorm = sb("rnorm", [P, 2, NH])
        qT = sb("qT", [P, PAIRS, P])
        kT = sb("kT", [P, PAIRS, 2, WIN + P])
        vtile = sb("vtile", [P, 4, INNER])
        vwin = sb("vwin", [P, NWIN, 2, PAIRS, HD])
        mx = sb("mx", [P, NH])
        shifted = sb("shifted", [P, NH * KEYS])
        prob = sb("probD", [P, NH * KEYS])
        den = sb("den", [P, NH])
        rden = sb("rdenD", [P, NH])
        pT = sb("pT", [P, PAIRS, P])
        on = sb("on", [P, INNER])
        oT = sb("oT", [P, PAIRS, P])
        yc = sb("yc", [P, P])
        ysq = sb("ysq", [P, P])
        std = sb("stdD", [P, P])
        rstd = sb("rstdD", [P, P])
        yn0 = sb("yn0", [P, P])
        yn = sb("yn", [P, P])
        gate = sb("gate", [P, FFT, P])
        hid = sb("hid", [P, FFT, P])
        big = [ctx.enter_context(nc.psum_tensor(f"big{n}", [P, 2 * BANK], F32)) for n in range(3)]
        small = [ctx.enter_context(nc.psum_tensor(f"small{n}", [P, BANK], F32)) for n in range(2)]

        par, cst = sem("par"), sem("cst")
        w_qkv, w_o, w_1, w_2, vmoved = sem("w_qkv"), sem("w_o"), sem("w_1"), sem("w_2"), sem("vmoved")
        g_memset, v_memset, v_cst = sem("g_memset"), sem("v_memset"), sem("v_cst")
        (p_tq, p_tk, p_ot, p_q, p_mu, p_k, p_wo, p_v, p_var, p_pt, p_gate, p_a, p_s, p_pv, p_w2) = (
            sem(f"p_{n}") for n in ("tq", "tk", "otD", "q", "mu", "k", "wo", "vD", "var", "pt", "gate", "a", "s",
                                    "pvD", "w2"))
        (a_carry, a_qT, a_kT, a_oT, a_sqq, a_sqk, a_v, a_norm, a_std, a_pT, a_gelu, a_exp) = (
            sem(f"a_{n}") for n in ("carry", "qT", "kT", "oT", "sqq", "sqk", "vD", "norm", "stdD", "pT", "gelu", "expD"))
        (v_q, v_yc, v_ysq, v_ssq, v_k, v_ssk, v_clamp, v_rk, v_y, v_rstd, v_yn0, v_yn, v_hid, v_max, v_sub,
         v_on, v_den, v_rden, v_x) = (
            sem(f"v_{n}") for n in ("q", "yc", "ysq", "ssq", "k", "ssk", "clamp", "rk", "y", "rstdD", "yn0",
                                    "yn", "hid", "max", "sub", "on", "den", "rdenD", "x"))
        (g_addq, g_mulq, g_addk, g_mulk, g_xs, g_tab, g_ys) = (
            sem(f"g_{n}") for n in ("addq", "mulq", "addk", "mulk", "xs", "tab", "ys"))

        block = ctx.enter_context(nc.Block())
        NPAR, NQKV, NO, N1, N2, NVM = 15 * DEPTH, 5, 2, 2, FFT, 10

        def pipeline(eng, step):
            for i in range(LAST):
                step(i)
            with eng.Fori(LAST, STEPS) as i:
                step(i)
            for i in range(STEPS, STEPS + LAST):
                step(i)

        def on_tile(i, lag):
            n = i - lag
            return None if isinstance(n, int) and not 0 <= n < STEPS else n

        def upto(value):
            return min(value, STEPS) if isinstance(value, int) else value

        @block.sync
        def _(sp):
            def load_qkv(l):
                whole = wqkv[:, bass.ds(l & 1, 1), :].rearrange("f o d -> f (o d)")
                for part in range(2):
                    src = lqkv[l, :, part * INNER:(part + 1) * INNER].rearrange("f (s p d) -> f s p d", s=2, d=HD)
                    dst = whole[:, part * INNER:(part + 1) * INNER].rearrange("f (p s d) -> f s p d", s=2, d=HD)
                    for s in range(2):
                        sp.dma_start(dst[:, s], src[:, s]).then_inc(w_qkv, 16)
                sp.dma_start(whole[:, 2 * INNER:], lqkv[l, :, 2 * INNER:]).then_inc(w_qkv, 16)

            def load_o(l):
                src = lwo[l].rearrange("(s p d) n -> s d p n", s=2, d=HD)
                for s in range(2):
                    sp.dma_start(wo_sb[s * HD:(s + 1) * HD], src[s]).then_inc(w_o, 16)

            def load_1(l):
                for a in range(2):
                    sp.dma_start(w1_sb[:, a, 0:FF], lw1[l, :, a * FF:(a + 1) * FF]).then_inc(w_1, 16)

            def load_2(l):
                for j in range(FFT):
                    rows = P if j < FFT - 1 else FFL
                    sp.dma_start(w2_sb[0:rows, j, :], lw2[l, j * P:j * P + rows, :]).then_inc(w_2, 16)

            def move_v(n, r, first=False):
                if first:
                    sp.wait_ge(a_v, n + 1)
                else:
                    sp.wait_ge(p_pv, n)
                sp.wait_ge(g_memset, 2)
                old = (r + 3) & 3
                cur, prev = vtile[:, r:r + 1, :], vtile[:, old:old + 1, :]
                for s in range(2):
                    half = slice(s * PAIRS * HD, (s + 1) * PAIRS * HD)
                    row = s * KEYS
                    dst = vwin[:].rearrange("p c s q d -> p c s (q d)")
                    sp.dma_start(dst[row:row + WIN, 0:1, s, :], prev[P - WIN:P, :, half]).then_inc(vmoved, 16)
                    sp.dma_start(dst[row + WIN:row + KEYS, 0:1, s, :], cur[0:WIN, :, half]).then_inc(vmoved, 16)
                    for c in range(1, NWIN):
                        sp.dma_start(dst[row:row + KEYS, c:c + 1, s, :],
                                     cur[WIN * (c - 1):WIN * (c + 1), :, half]).then_inc(vmoved, 16)

            def layer(l, more):
                for t in (-1, 0):
                    move_v(l * TILES + t, t & 3)
                if more:
                    load_qkv(l + 1)
                sp.wait_ge(p_wo, l * TILES)
                load_o(l)
                move_v(l * TILES + 1, 1)
                sp.wait_ge(p_a, l * TILES)
                load_1(l)
                move_v(l * TILES + 2, 2)
                sp.wait_ge(p_w2, l * TILES)
                load_2(l)
                with sp.Fori(0, 3) as g:
                    for t in range(3, 7):
                        move_v(l * TILES + g * 4 + t, t & 3)

            load_qkv(0)
            load_o(0)
            sp.wait_ge(v_memset, 4)
            load_1(0)
            load_2(0)
            sp.wait_ge(w_qkv, NQKV * 16)
            load_qkv(1)
            move_v(0, 0, first=True)
            for t in (1, 2):
                move_v(t, t)
            with sp.Fori(0, 3) as g:
                for t in range(3, 7):
                    move_v(g * 4 + t, t & 3)
            with sp.Fori(1, DEPTH - 1) as l:
                layer(l, True)
            layer(DEPTH - 1, False)
            move_v(STEPS - 1, 3)
            sp.wait_ge(vmoved, NVM * 16 * STEPS)

        @block.gpsimd
        def _(pool):
            pool.dma_start(rope_sb[:], rope).then_inc(cst, 16)
            pool.dma_start(cscale[:], carry_scale).then_inc(cst, 16)
            pool.dma_start(mask_f[:], mask).then_inc(cst, 16)
            pool.memset(vwin[:], 0.0).then_inc(g_memset, 1)
            pool.memset(vtile[:, 3, :], 0.0).then_inc(g_memset, 1)
            pool.memset(Y[:, 0:1], 0.0).then_inc(g_memset, 1)
            pool.wait_ge(cst, 48)
            pool.wait_ge(par, NPAR * 16)
            pool.wait_ge(v_memset, 4)

            def shift(dst, src, t, before, done, n):
                at = t * P
                pool.tensor_copy(dst[0:P // 2, :], src[0:P // 2, bass.ds(at + 1, P)])
                for s_before, value in before:
                    need(pool, s_before, value)
                pool.tensor_copy(dst[P // 2:P, :], src[P // 2:P, bass.ds(at, P)]).then_inc(done, 1)
                pool.wait_ge(done, n + 1)

            def prepare(n, before):
                t, l = n & (TILES - 1), layer_of(n)
                need(pool, p_v, n)
                shift(xs, X, t, before, g_xs, n)
                need(pool, v_k, n)
                src = rope_sb[:, bass.ds(t, 1), :, :].rearrange("p o k d -> p (o k) d")
                fac = scales[:, bass.ds(l, 1), :, :].rearrange("p o k d -> p (o k) d")
                pool.tensor_tensor(tab[:], src, fac, ALU.mult).then_inc(g_tab, 1)

            def step(i):
                if (n := on_tile(i, 0)) is not None:
                    for part, (done, add) in enumerate(((v_q, g_addq), (v_k, g_addk))):
                        pool.wait_ge(done, n + 1)
                        pool.tensor_tensor(rot[:, part], rot[:, part], rot2[:, part], ALU.add).then_inc(add, 1)
                if (n := on_tile(i, -1)) is not None:
                    prepare(n, [(g_addk, n)])
                if (n := on_tile(i, 0)) is not None:
                    pool.wait_ge(v_rk, n + 1)
                    for part, (add, turned, mul) in enumerate(((g_addq, p_tq, g_mulq), (g_addk, p_tk, g_mulk))):
                        pool.wait_ge(add, n + 1)
                        need(pool, turned, n)
                        pool.tensor_tensor(rotn[:, part].rearrange("p (h d) -> p h d", d=HD),
                                           rot[:, part].rearrange("p (h d) -> p h d", d=HD),
                                           rnorm[:, part].unsqueeze(2).broadcast_to([P, NH, HD]),
                                           ALU.mult).then_inc(mul, 1)
                if (n := on_tile(i, 3)) is not None:
                    pool.wait_ge(v_y, n + 1)
                    need(pool, v_yc, n)
                    shift(ys, Y, n & (TILES - 1), [(g_mulk, upto(i + 1))], g_ys, n)

            prepare(0, [(g_memset, 3)])
            for i in range(LAST):
                step(i)
            with pool.Fori(LAST, STEPS - 1) as i:
                step(i)
            for i in range(STEPS - 1, STEPS + LAST):
                step(i)

        @block.vector
        def _(dve):
            dve.memset(b1col[:], 0.0).then_inc(v_memset, 1)
            dve.memset(w1_sb[:], 0.0).then_inc(v_memset, 1)
            dve.memset(w2_sb[:], 0.0).then_inc(v_memset, 1)
            dve.memset(eps[:], EPS)
            dve.memset(kT[:], 0.0).then_inc(v_memset, 1)
            dve.memset(mean_w[:], 1.0 / DIM).then_inc(v_memset, 1)
            dve.wait_ge(cst, 48)
            dve.tensor_copy(mask_b[:], mask_f[:]).then_inc(v_cst, 1)
            dve.tensor_copy(ident_b[:], ident[:]).then_inc(v_cst, 1)
            dve.wait_ge(par, NPAR * 16)
            dve.wait_ge(g_memset, 3)

            def rotate(part, ps):
                x3 = ps[:].rearrange("p (h d) -> p h d", d=HD)
                r1 = rot[:, part].rearrange("p (h d) -> p h d", d=HD)
                r2 = rot2[:, part].rearrange("p (h d) -> p h d", d=HD)
                half = HD // 2
                dve.tensor_tensor(r1, x3, tab[:, 2 * part].unsqueeze(1).broadcast_to([P, NH, HD]), ALU.mult)
                for a, b in ((0, half), (half, 0)):
                    last = dve.tensor_tensor(r2[:, :, a:a + half], x3[:, :, b:b + half],
                                             tab[:, 2 * part + 1, a:a + half].unsqueeze(1)
                                             .broadcast_to([P, NH, half]), ALU.mult)
                return last

            def sum_squares(part, n, squares, s_sum):
                dve.wait_ge(squares, n + 1)
                dve.tensor_reduce(ssum[:, part], sq[:, part].rearrange("p (h d) -> p h d", d=HD), AX.X,
                                  ALU.add).then_inc(s_sum, 1)

            def step(i):
                if (n := on_tile(i, 4)) is not None:
                    dve.wait_ge(p_mu, n + 1)
                    dve.tensor_tensor(yc[:], small[1][:, 0:P], ys[:], ALU.subtract).then_inc(v_yc, 1)
                    dve.wait_ge(v_yc, n + 1)
                    need(dve, p_var, n)
                    dve.tensor_tensor(ysq[:], yc[:], yc[:], ALU.mult).then_inc(v_ysq, 1)
                if (n := on_tile(i, 0)) is not None:
                    dve.wait_ge(a_sqq, n + 1)
                    dve.wait_ge(g_tab, n + 1)
                    need(dve, g_mulq, n)
                    rotate(0, big[0]).then_inc(v_q, 1)
                if (n := on_tile(i, 5)) is not None:
                    l = layer_of(n)
                    dve.wait_ge(p_w2, n + 1)
                    cols = bass.ds((n & (TILES - 1)) * P + 1, P)
                    dve.scalar_tensor_tensor(out=X[:, cols], in0=small[0][:, 0:P], scalar=b2col[:, bass.ds(l, 1)],
                                             in1=Y[:, cols], op0=ALU.add, op1=ALU.add).then_inc(v_x, 1)
                if (n := on_tile(i, 0)) is not None:
                    dve.wait_ge(a_sqk, n + 1)
                    need(dve, g_mulk, n)
                    rotate(1, big[1]).then_inc(v_k, 1)
                    sum_squares(0, n, a_sqq, v_ssq)
                    sum_squares(1, n, a_sqk, v_ssk)
                    dve.wait_ge(v_ssk, n + 1)
                    need(dve, a_norm, n)
                    dve.tensor_scalar(clamped[:], ssum[:], 1e-24, None, ALU.max).then_inc(v_clamp, 1)
                if (n := on_tile(i, 2)) is not None:
                    dve.wait_ge(a_exp, n + 1)
                    dve.tensor_reduce(den[:], prob[:].rearrange("p (h k) -> p h k", k=KEYS), AX.X,
                                      ALU.add).then_inc(v_den, 1)
                    dve.wait_ge(v_den, n + 1)
                    dve.reciprocal(rden[:], den[:]).then_inc(v_rden, 1)
                if (n := on_tile(i, 3)) is not None:
                    dve.wait_ge(p_wo, n + 1)
                    cols = bass.ds((n & (TILES - 1)) * P + 1, P)
                    dve.tensor_tensor(Y[:, cols], small[0][:, 0:P], X[:, cols], ALU.add).then_inc(v_y, 1)
                if (n := on_tile(i, 0)) is not None:
                    dve.wait_ge(a_norm, n + 1)
                    need(dve, g_mulk, n)
                    dve.reciprocal(rnorm[:], norm[:]).then_inc(v_rk, 1)
                if (n := on_tile(i, 4)) is not None:
                    l = layer_of(n)
                    dve.wait_ge(a_std, n + 1)
                    dve.reciprocal(rstd[:], std[:]).then_inc(v_rstd, 1)
                    dve.wait_ge(v_rstd, n + 1)
                    dve.scalar_tensor_tensor(out=yn0[:], in0=yc[:], scalar=-1.0, in1=rstd[:], op0=ALU.mult,
                                             op1=ALU.mult).then_inc(v_yn0, 1)
                    dve.wait_ge(v_yn0, n + 1)
                    need(dve, p_a, n)
                    dve.tensor_scalar(yn[:], yn0[:], gcol[:, bass.ds(l, 1)], bcol[:, bass.ds(l, 1)], ALU.mult,
                                      ALU.add).then_inc(v_yn, 1)
                if (n := on_tile(i, 1)) is not None:
                    s3 = big[1][:].rearrange("p (h k) -> p h k", k=KEYS)
                    dve.wait_ge(p_s, n + 1)
                    dve.tensor_reduce(mx[:], s3, AX.X, ALU.max).then_inc(v_max, 1)
                    dve.wait_ge(v_max, n + 1)
                    need(dve, a_exp, n)
                    dve.tensor_tensor(shifted[:].rearrange("p (h k) -> p h k", k=KEYS), s3,
                                      mx[:].unsqueeze(2).broadcast_to([P, NH, KEYS]), ALU.subtract)\
                       .then_inc(v_sub, 1)
                if (n := on_tile(i, 2)) is not None:
                    dve.wait_ge(p_pv, n + 1)
                    dve.wait_ge(v_rden, n + 1)
                    need(dve, p_ot, n)
                    dve.tensor_tensor(on[:].rearrange("p (h d) -> p h d", d=HD),
                                      big[2][:].rearrange("p (h d) -> p h d", d=HD),
                                      rden[:].unsqueeze(2).broadcast_to([P, NH, HD]), ALU.mult).then_inc(v_on, 1)
                if (n := on_tile(i, 4)) is not None:
                    l = layer_of(n)
                    dve.wait_ge(p_a, n + 1)
                    dve.wait_ge(a_gelu, n + 1)
                    need(dve, p_w2, n)
                    for j in range(FFT):
                        last = dve.scalar_tensor_tensor(
                            out=hid[:, j, :], in0=small[0][:, j * P:(j + 1) * P],
                            scalar=b1col[:, 0, j, bass.ds(l, 1)], in1=gate[:, j, :], op0=ALU.add, op1=ALU.mult)
                    last.then_inc(v_hid, 1)

            pipeline(dve, step)
            dve.wait_ge(v_x, STEPS)

        @block.scalar
        def _(act):
            for l in range(DEPTH):
                half = HD // 2
                for k, vec in ((0, lqs), (2, lks)):
                    row = vec[l].rearrange("(o d) -> o d", o=1)
                    act.dma_start(scales[:, l, k, :], row.broadcast_to([P, HD])).then_inc(par, 16)
                    for a, b in ((0, half), (half, 0)):
                        act.dma_start(scales[:, l, k + 1, a:a + half],
                                      row[:, b:b + half].broadcast_to([P, half])).then_inc(par, 16)
                for col, vec in ((gcol, lg), (bcol, lb), (b2col, lb2)):
                    act.dma_start(col[:, l:l + 1], vec[l].rearrange("(d o) -> d o", o=1)).then_inc(par, 16)
            act.wait_ge(v_memset, 4)
            for l in range(DEPTH):
                for a in range(2):
                    for j in range(FFT):
                        rows = P if j < FFT - 1 else FFL
                        src = lb1[l, a * FF + j * P:a * FF + j * P + rows].rearrange("(d o) -> d o", o=1)
                        act.dma_start(b1col[0:rows, a, j, l:l + 1], src).then_inc(par, 16)
            act.wait_ge(par, NPAR * 16)
            act.wait_ge(cst, 48)

            def copy(dst, src):
                return act.activation(dst, src, ACT.Copy)

            def step(i):
                if (n := on_tile(i, 1)) is not None:
                    need(act, p_s, n)
                    need(act, a_kT, n)
                    act.activation(kT[:, :, :, 0:WIN], kT[:, :, :, P:P + WIN], ACT.Copy,
                                   scale=cscale[:, 0:1]).then_inc(a_carry, 1)
                if (n := on_tile(i, 0)) is not None:
                    act.wait_ge(p_q, n + 1)
                    need(act, v_ssq, n)
                    act.activation(sq[:, 0], big[0][:], ACT.Square).then_inc(a_sqq, 1)
                if (n := on_tile(i, 3)) is not None:
                    act.wait_ge(p_ot, n + 1)
                    need(act, p_wo, n)
                    copy(oT[:].rearrange("p q t -> p (q t)"), big[2][:]).then_inc(a_oT, 1)
                if (n := on_tile(i, 0)) is not None:
                    act.wait_ge(p_k, n + 1)
                    need(act, v_ssk, n)
                    act.activation(sq[:, 1], big[1][:], ACT.Square).then_inc(a_sqk, 1)
                if (n := on_tile(i, 1)) is not None:
                    act.wait_ge(p_tk, n + 1)
                    act.wait_ge(a_carry, n + 1)
                    for s in range(2):
                        rows = slice(s * HD, (s + 1) * HD)
                        last = copy(kT[rows, :, s, WIN:WIN + P], big[2][rows].rearrange("p (q t) -> p q t", t=P))
                    last.then_inc(a_kT, 1)
                if (n := on_tile(i, 2)) is not None:
                    act.wait_ge(p_pt, n + 1)
                    need(act, p_pv, n)
                    copy(pT[:].rearrange("p q t -> p (q t)"), big[0][:]).then_inc(a_pT, 1)
                if (n := on_tile(i, 0)) is not None:
                    act.wait_ge(p_v, n + 1)
                    need(act, vmoved, (n - 2) * (NVM * 16))
                    copy(vtile[:, bass.ds(n & 3, 1), :].rearrange("p o d -> p (o d)"), big[2][:]).then_inc(a_v, 1)
                if (n := on_tile(i, 1)) is not None:
                    act.wait_ge(p_tq, n + 1)
                    copy(qT[:].rearrange("p q t -> p (q t)"), big[0][:]).then_inc(a_qT, 1)
                if (n := on_tile(i, 0)) is not None:
                    act.wait_ge(v_clamp, n + 1)
                    need(act, v_rk, n)
                    act.activation(norm[:], clamped[:], ACT.Sqrt).then_inc(a_norm, 1)
                if (n := on_tile(i, 4)) is not None:
                    act.wait_ge(p_var, n + 1)
                    need(act, v_rstd, n)
                    act.activation(std[:], small[1][:, 0:P], ACT.Sqrt, bias=eps[:, 0:1]).then_inc(a_std, 1)
                if (n := on_tile(i, 1)) is not None:
                    act.wait_ge(v_sub, n + 1)
                    need(act, p_pt, n)
                    need(act, v_den, n)
                    act.activation(prob[:], shifted[:], ACT.Exp).then_inc(a_exp, 1)
                if (n := on_tile(i, 4)) is not None:
                    act.wait_ge(p_gate, n + 1)
                    need(act, v_hid, n)
                    for j in range(FFT):
                        last = act.activation(gate[:, j, :], small[1][:, j * P:(j + 1) * P], ACT.Gelu,
                                              bias=b1col[:, 1, j, bass.ds(layer_of(n), 1)])
                    last.then_inc(a_gelu, 1)

            pipeline(act, step)

        @block.tensor
        def _(pe):
            pe.wait_ge(v_memset, 5)
            pe.wait_ge(v_cst, 2)

            def turn(ps, src):
                for p in range(PAIRS):
                    last = pe.transpose(ps[:, p * P:(p + 1) * P], src[:, p * P:(p + 1) * P], ident[:])
                return last

            def project(ps, part, l):
                w = wqkv[:, bass.ds(l & 1, 1), :].rearrange("f o d -> f (o d)")
                for h in range(2):
                    at = part * INNER + h * BANK
                    last = pe.matmul(ps[:, h * BANK:(h + 1) * BANK], xs[:], w[:, at:at + BANK],
                                     start=True, stop=True)
                return last

            def step(i):
                if (n := on_tile(i, 0)) is not None:
                    pe.wait_ge(g_xs, n + 1)
                    pe.wait_ge(w_qkv, (layer_of(n) + 1) * (NQKV * 16))
                    need(pe, a_qT, n - 1)
                    project(big[0], 0, layer_of(n)).then_inc(p_q, 1)
                if (n := on_tile(i, 3)) is not None:
                    pe.wait_ge(v_on, n + 1)
                    turn(big[2], on).then_inc(p_ot, 1)
                if (n := on_tile(i, 4)) is not None:
                    pe.wait_ge(g_ys, n + 1)
                    need(pe, a_gelu, n)
                    pe.matmul(small[1][:, 0:P], mean_w[:], ys[:], start=True, stop=True).then_inc(p_mu, 1)
                if (n := on_tile(i, 0)) is not None:
                    need(pe, v_sub, n - 1)
                    project(big[1], 1, layer_of(n)).then_inc(p_k, 1)
                if (n := on_tile(i, 4)) is not None:
                    pe.wait_ge(v_ysq, n + 1)
                    pe.matmul(small[1][:, 0:P], mean_w[:], ysq[:], start=True, stop=True).then_inc(p_var, 1)
                if (n := on_tile(i, 1)) is not None:
                    pe.wait_ge(g_mulk, n + 1)
                    need(pe, a_oT, i - 2)
                    turn(big[2], rotn[:, 1]).then_inc(p_tk, 1)
                if (n := on_tile(i, 5)) is not None:
                    pe.wait_ge(v_hid, n + 1)
                    pe.wait_ge(w_2, (layer_of(n) + 1) * (N2 * 16))
                    for j in range(FFT):
                        last = pe.matmul(small[0][:, 0:P], w2_sb[:, j, :], hid[:, j, :],
                                         start=(j == 0), stop=(j == FFT - 1))
                    last.then_inc(p_w2, 1)
                if (n := on_tile(i, 2)) is not None:
                    pe.wait_ge(a_exp, n + 1)
                    pe.wait_ge(v_q, upto(i + 1))
                    need(pe, a_qT, upto(i - 1))
                    turn(big[0], prob).then_inc(p_pt, 1)
                if (n := on_tile(i, 0)) is not None:
                    need(pe, a_kT, i)
                    project(big[2], 2, layer_of(n)).then_inc(p_v, 1)
                if (n := on_tile(i, 1)) is not None:
                    need(pe, v_q, upto(i + 1))
                    need(pe, a_pT, i - 1)
                    turn(big[0], rotn[:, 0]).then_inc(p_tq, 1)
                if (n := on_tile(i, 3)) is not None:
                    pe.wait_ge(a_oT, n + 1)
                    pe.wait_ge(w_o, (layer_of(n) + 1) * (NO * 16))
                    need(pe, v_x, n - 1)
                    for p in range(PAIRS):
                        last = pe.matmul(small[0][:, 0:P], wo_sb[:, p, :], oT[:, p, :],
                                         start=(p == 0), stop=(p == PAIRS - 1))
                    last.then_inc(p_wo, 1)
                if (n := on_tile(i, 1)) is not None:
                    pe.wait_ge(a_qT, n + 1)
                    pe.wait_ge(a_kT, n + 1)
                    pe.wait_ge(v_k, upto(i + 1))
                    need(pe, v_sub, i - 1)
                    first = ((n & (TILES - 1)) + TILES - 1) >> 4
                    if not isinstance(n, int):
                        first = first.with_bounds(min_val=0, max_val=1)
                    m = mask_b[:, bass.ds(first, 1), :].broadcast_to([P, PAIRS, KEYS])
                    for h in range(2):
                        pe.matmul(big[1][:, h * BANK:(h + 1) * BANK].rearrange("p (h k) -> p h k", k=KEYS),
                                  ident_b[:], m, start=True, stop=False, skip_group_check=True)
                    for p in range(PAIRS):
                        for c in range(NWIN):
                            rows = slice(c * WIN, (c + 1) * WIN)
                            last = pe.matmul(big[1][rows, p * P:(p + 1) * P], qT[:, p, rows],
                                             kT[:, p, :, c * WIN:c * WIN + KEYS], start=False, stop=True,
                                             skip_group_check=True)
                    last.then_inc(p_s, 1)
                if (n := on_tile(i, 2)) is not None:
                    pe.wait_ge(a_pT, n + 1)
                    pe.wait_ge(vmoved, (n + 1) * (NVM * 16))
                    pe.wait_ge(a_v, upto(i + 1))
                    need(pe, a_kT, upto(i))
                    need(pe, a_oT, upto(i - 2))
                    for p in range(PAIRS):
                        for c in range(NWIN):
                            rows = slice(c * WIN, (c + 1) * WIN)
                            last = pe.matmul(big[2][rows, p * P:(p + 1) * P], pT[:, p, rows], vwin[:, c, :, p, :],
                                             start=True, stop=True, skip_group_check=True)
                    last.then_inc(p_pv, 1)
                if (n := on_tile(i, 4)) is not None:
                    pe.wait_ge(v_yn, n + 1)
                    pe.wait_ge(w_1, (layer_of(n) + 1) * (N1 * 16))
                    need(pe, v_y, upto(i - 2))
                    for ps, a, done in ((small[1], 1, p_gate), (small[0], 0, p_a)):
                        for j in range(FFT):
                            last = pe.matmul(ps[:, j * P:(j + 1) * P], w1_sb[:, a, j * P:(j + 1) * P], yn[:],
                                             start=True, stop=True)
                        last.then_inc(done, 1)

            pipeline(pe, step)


def stage_e(nc, x, ident, X, att, out):
    with ExitStack() as ctx:
        def sem(name):
            return ctx.enter_context(nc.semaphore(name))

        xin = ctx.enter_context(nc.sbuf_tensor("xinE", [P, TILES, DIM], F32))
        g = ctx.enter_context(nc.sbuf_tensor("gE", [P, SEQ], F32))
        z = ctx.enter_context(nc.sbuf_tensor("zE", [P, SEQ], F32))
        res = ctx.enter_context(nc.sbuf_tensor("resE", [P, TILES, DIM], F32))
        ps = ctx.enter_context(nc.psum_tensor("psE", [P, 4, BANK], F32))
        x_in, stored, a_g, v_z, p_z, v_res = (sem(n) for n in ("x_inE", "storedE", "a_g", "v_z", "p_z", "v_res"))
        block = ctx.enter_context(nc.Block())

        @block.sync
        def _(sp):
            sp.dma_start(xin[:], x[0].rearrange("(t p) d -> p t d", p=P)).then_inc(x_in, 16)
            rows = out[0].rearrange("(t p) d -> p t d", p=P)
            for c in range(4):
                sp.wait_ge(v_res, c + 1)
                sp.dma_start(rows[:, 4 * c:4 * c + 4], res[:, 4 * c:4 * c + 4]).then_inc(stored, 16)
            sp.wait_ge(stored, 64)

        @block.scalar
        def _(act):
            for c in range(4):
                act.activation(g[:, c * BANK:(c + 1) * BANK], X[:, 1 + c * BANK:1 + (c + 1) * BANK],
                               ACT.Silu).then_inc(a_g, 1)

        @block.vector
        def _(dve):
            dve.wait_ge(x_in, 16)
            for c in range(4):
                cols = slice(c * BANK, (c + 1) * BANK)
                dve.wait_ge(a_g, c + 1)
                dve.tensor_tensor(z[:, cols], att[:, cols], g[:, cols], ALU.mult).then_inc(v_z, 1)
            for c in range(4):
                dve.wait_ge(p_z, c + 1)
                dve.tensor_tensor(res[:, 4 * c:4 * c + 4], ps[:, c, :].rearrange("p (t d) -> p t d", t=4),
                                  xin[:, 4 * c:4 * c + 4], ALU.add).then_inc(v_res, 1)

        @block.tensor
        def _(pe):
            for t in range(TILES):
                if t % 4 == 0:
                    pe.wait_ge(v_z, t // 4 + 1)
                last = pe.transpose(ps[:, t // 4, t % 4 * P:(t % 4 + 1) * P], z[:, t * P:(t + 1) * P], ident[:])
                if t % 4 == 3:
                    last.then_inc(p_z, 1)


def shape_tables():
    f = np.float32
    half = np.arange(0, HD, 2, dtype=f)
    inv_freq = (f(1) / f(10000) ** (half / f(HD))).astype(f)
    angle = np.arange(SEQ, dtype=f)[:, None] * inv_freq[None, :]
    angle = np.concatenate([angle, angle], -1).astype(np.float64)
    base = ((half + 0.4 * HD) / (1.4 * HD)).astype(f).astype(np.float64)
    base = np.concatenate([base, base])
    power = (np.arange(SEQ) % P - P // 2) / (WIN // 2)
    scale = base[None, :] ** power[:, None]
    sign = np.where(np.arange(HD) < HD // 2, -1.0, 1.0)
    cos, sin = np.cos(angle), np.sin(angle) * sign
    rope = np.stack([8.0 * cos * scale, 8.0 * sin * scale, cos / scale, sin / scale], 1)
    rope = rope.reshape(TILES, P, 4, HD).transpose(1, 0, 2, 3).astype(f)
    carry = np.tile(base ** (P / (WIN // 2)), 2).reshape(P, 1).astype(f)
    row, key = np.arange(P)[:, None] % WIN, np.arange(KEYS)[None, :]
    ok = (row <= key) & (key <= row + WIN)
    first = ok & ((np.arange(P)[:, None] >= WIN) | (key >= WIN))
    mask = np.where(np.stack([first, ok], 1), 0.0, -1e30).astype(f)
    return {"rope": np.ascontiguousarray(rope), "carry_scale": carry, "mask": mask, "eye": np.eye(P, dtype=f)}


_INS = ["L0_attn_x", "L0_attn_Wv", "L0_attn_Wk", "L0_attn_Wq", "L0_attn_Wo", "L0_attn_bo", "L0_ffn_Wqkv",
        "L0_ffn_q_scale", "L0_ffn_k_scale", "L0_ffn_Wo", "L0_ffn_ln_g", "L0_ffn_ln_b", "L0_ffn_W1", "L0_ffn_b1",
        "L0_ffn_W2", "L0_ffn_b2"]


def kernel(**inputs):
    import concourse.bacc as _bacc
    from concourse.bass_utils import run_bass_kernel_spmd as _run

    nc = _bacc.Bacc("TRN2", target_bir_lowering=False, num_devices=1)
    arrays, args = {}, []
    tables = shape_tables()
    for name in _INS + list(tables):
        a = np.ascontiguousarray(tables[name] if name in tables else inputs[name])
        arrays[f"in_{name}"] = a
        args.append(nc.dram_tensor(f"in_{name}", a.shape, mybir.dt.from_np(a.dtype), kind="ExternalInput").ap())
    out = nc.dram_tensor("out_0", (1, SEQ, DIM), F32, kind="ExternalOutput").ap()
    build(nc, *args, out)
    r = _run(nc, [arrays], core_ids=[0])
    return r.results[0]["out_0"]
```

```python
from contextlib import ExitStack

import numpy as np

import concourse.bass as bass
from concourse import mybir

F32 = mybir.dt.float32
F32R = mybir.dt.float32r
BF16 = mybir.dt.bfloat16
ALU = mybir.AluOpType
ACT = mybir.ActivationFunctionType
AX = mybir.AxisListType

P = 128
SEQ = 2048
DIM = 128
TILES = SEQ // P
BANK = 512

GH = 16
GD = DIM // GH
SPLIT = 4 * GD
GBUF = 4
MAXSTEP = 13
RING = 3
ROUND = 4 * (4 * TILES + 2)
LEAD = 20
PSLOTS = 8
PVLAG = 2
VCOL = 32

DEPTH = 6
NH = 16
HD = 64
PAIRS = NH // 2
WIN = 32
NWIN = P // WIN
KEYS = 2 * WIN
INNER = NH * HD
FF = int(DIM * 4 * 2 / 3)
FFT = 3
FFL = FF - (FFT - 1) * P
STEPS = DEPTH * TILES
EPS = 1e-5
LAST = 5


def need(eng, sem, value):
    if not isinstance(value, int) or value > 0:
        eng.wait_ge(sem, value)


def layer_of(n):
    l = n // TILES if isinstance(n, int) else (n >> 4)
    return l if isinstance(n, int) else l.with_bounds(min_val=0, max_val=DEPTH - 1)


def build(nc, x, wv, wk, wq, wo, bo, lqkv, lqs, lks, lwo, lg, lb, lw1, lb1, lw2, lb2,
          rope, carry_scale, mask, eye, out):
    scratch = nc.dram_tensor("split_operands", [4, DIM, SEQ], F32, kind="Internal").ap()
    att_scratch = nc.dram_tensor("attention", [P, SEQ], F32, kind="Internal").ap()
    max_scratch = nc.dram_tensor("maxima", [2, TILES, P], F32, kind="Internal").ap()
    persistent = ExitStack()

    def keep(name, shape, dt=F32):
        return persistent.enter_context(nc.sbuf_tensor(name, shape, dt))

    with persistent:
        ident = keep("ident", [P, P])
        X = keep("X", [P, 1 + SEQ])
        small = {
            "scales": keep("scales", [P, 4, DEPTH, HD]),
            "gcol": keep("gcol", [P, DEPTH]),
            "bcol": keep("bcol", [P, DEPTH]),
            "b2col": keep("b2col", [P, DEPTH]),
            "b1col": keep("b1col", [P, 2, FFT, DEPTH]),
            "rope_sb": keep("rope_sb", [P, TILES, 4, HD]),
            "cscale": keep("cscale", [P, 1]),
            "mask_f": keep("mask_f", [P, 2, KEYS]),
        }
        with ExitStack() as ctx:
            vtok = ctx.enter_context(nc.sbuf_tensor("vtok", [P, TILES, DIM], F32))
            otok = ctx.enter_context(nc.sbuf_tensor("otok", [P, TILES, DIM], F32))
            wout = ctx.enter_context(nc.sbuf_tensor("wout", [P, DIM], F32))
            bout = ctx.enter_context(nc.sbuf_tensor("bout", [P, 1], F32))
            with ExitStack() as operands:
                qs, ks = (operands.enter_context(nc.sbuf_tensor(n, [P, GBUF, SEQ], F32R)) for n in ("qs", "ks"))
                stage_a(nc, x, wq, wk, wv, wo, bo, eye, scratch, ident, X, vtok, wout, bout, qs, ks)
                stage_b(nc, scratch, max_scratch, ident, vtok, otok, qs, ks, small,
                        (lqs, lks, lg, lb, lb1, lb2, rope, carry_scale, mask))
            stage_c(nc, ident, otok, wout, bout, att_scratch)
        stage_d(nc, lqkv, lwo, lw1, lw2, small, ident, X)
        stage_e(nc, x, ident, X, att_scratch, out)


def stage_a(nc, x, wq, wk, wv, wo, bo, eye, scratch, ident, X, vtok, wout, bout, qs, ks):
    with ExitStack() as ctx:
        def sb(name, shape, dt=F32):
            return ctx.enter_context(nc.sbuf_tensor(name, shape, dt))

        def sem(name):
            return ctx.enter_context(nc.semaphore(name))

        xin = sb("xin", [P, TILES, DIM])
        xc = sb("xc", [P, TILES, DIM])
        sq = sb("sq", [P, TILES, DIM])
        mean = sb("mean", [P, TILES])
        std = sb("std", [P, TILES])
        rstd = sb("rstd", [P, TILES])
        w = sb("w_in", [P, 3, DIM])
        split = sb("split", [P, 4, SEQ], F32R)
        ps = ctx.enter_context(nc.psum_tensor("psA", [P, 8, BANK], F32))

        x_in, w_in, cst_in, stored = sem("x_in"), sem("w_in_s"), sem("cst_in"), sem("stored")
        v_sum, v_mean, v_xc, v_var, v_rstd, v_xn = (sem(f"v_{n}") for n in ("sum", "mean", "xc", "var", "rstd", "xn"))
        a_sq, p_xt, a_xt, p_qk, v_hi, v_lo, p_v, a_v = (
            sem(n) for n in ("a_sq", "p_xt", "a_xt", "p_qk", "v_hi", "v_lo", "p_v", "a_v"))
        g_zero, a_std = sem("g_zero"), sem("a_std")

        block = ctx.enter_context(nc.Block())

        @block.sync
        def _(sp):
            sp.dma_start(xin[:], x[0].rearrange("(t p) d -> p t d", p=P)).then_inc(x_in, 16)
            sp.dma_start(ident[:], eye).then_inc(cst_in, 16)
            for n, src in enumerate((wq, wk, wv)):
                sp.dma_start(w[:, n, :], src).then_inc(w_in, 16)
            sp.dma_start(wout[:], wo).then_inc(cst_in, 16)
            sp.dma_start(bout[:], bo.rearrange("(d a) -> d a", a=1)).then_inc(cst_in, 16)
            for n in range(4):
                sp.wait_ge(v_hi if n % 2 == 0 else v_lo, 4 * (n // 2 + 1))
                sp.dma_start(scratch[n], split[:, n, :].bitcast(F32)).then_inc(stored, 16)
            sp.wait_ge(stored, 64)

        @block.gpsimd
        def _(pool):
            pool.memset(X[:, 0:1], 0.0)
            pool.memset(ks[:].bitcast(F32), 0.0).then_inc(g_zero, 1)
            pool.wait_ge(g_zero, 1)
            pool.memset(ks[SPLIT:SPLIT + 2, :, :].bitcast(F32), 1.0)

        @block.vector
        def _(dve):
            for b in range(GBUF // 2):
                dve.memset(qs[:, b, :].bitcast(F32), 0.0)
            dve.wait_ge(x_in, 16)
            dve.tensor_reduce(mean[:], xin[:], AX.X, ALU.add).then_inc(v_sum, 1)
            dve.wait_ge(v_sum, 1)
            dve.tensor_scalar(mean[:], mean[:], 1.0 / DIM, None, ALU.mult).then_inc(v_mean, 1)
            dve.wait_ge(v_mean, 1)
            dve.tensor_tensor(xc[:], xin[:], mean[:].unsqueeze(2).broadcast_to([P, TILES, DIM]),
                              ALU.subtract).then_inc(v_xc, 1)
            dve.wait_ge(a_sq, 1)
            dve.tensor_reduce(rstd[:], sq[:], AX.X, ALU.add).then_inc(v_var, 1)
            dve.wait_ge(v_var, 1)
            dve.tensor_scalar(rstd[:], rstd[:], 1.0 / DIM, EPS, ALU.mult, ALU.add).then_inc(v_rstd, 1)
            dve.wait_ge(a_std, 1)
            dve.reciprocal(rstd[:], std[:]).then_inc(v_rstd, 1)
            dve.wait_ge(v_rstd, 2)
            dve.tensor_tensor(xc[:], xc[:], rstd[:].unsqueeze(2).broadcast_to([P, TILES, DIM]),
                              ALU.mult).then_inc(v_xn, 1)
            for b in range(GBUF // 2, GBUF):
                dve.memset(qs[:, b, :].bitcast(F32), 0.0)
            for m in range(8):
                n, c = m // 4, m % 4
                dve.wait_ge(p_qk, m + 1)
                hi, lo = split[:, 2 * n, c * BANK:(c + 1) * BANK], split[:, 2 * n + 1, c * BANK:(c + 1) * BANK]
                dve.tensor_copy(hi, ps[:, m, :]).then_inc(v_hi, 1)
                dve.wait_ge(v_hi, m + 1)
                dve.tensor_tensor(lo, ps[:, m, :], hi.bitcast(F32), ALU.subtract).then_inc(v_lo, 1)

        @block.scalar
        def _(act):
            act.wait_ge(v_xc, 1)
            act.activation(sq[:], xc[:], ACT.Square).then_inc(a_sq, 1)
            act.wait_ge(v_rstd, 1)
            act.activation(std[:], rstd[:], ACT.Sqrt).then_inc(a_std, 1)
            for c in range(4):
                act.wait_ge(p_xt, c + 1)
                act.activation(X[:, 1 + c * BANK:1 + (c + 1) * BANK], ps[:, c, :], ACT.Copy).then_inc(a_xt, 1)
            for c in range(4):
                act.wait_ge(p_v, c + 1)
                act.activation(vtok[:, 4 * c:4 * c + 4, :], ps[:, c, :].rearrange("p (t d) -> p t d", t=4),
                               ACT.Copy).then_inc(a_v, 1)

        @block.tensor
        def _(pe):
            pe.wait_ge(cst_in, 48)
            pe.wait_ge(v_xn, 1)
            for t in range(TILES):
                last = pe.transpose(ps[:, t // 4, t % 4 * P:(t % 4 + 1) * P], xc[:, t, :], ident[:])
                if t % 4 == 3:
                    last.then_inc(p_xt, 1)
            pe.wait_ge(w_in, 48)
            pe.wait_ge(a_xt, 4)
            for m in range(8):
                n, c = m // 4, m % 4
                pe.matmul(ps[:, m, :], w[:, n, :], X[:, 1 + c * BANK:1 + (c + 1) * BANK],
                          start=True, stop=True).then_inc(p_qk, 1)
            for t in range(TILES):
                if t % 4 == 0:
                    pe.wait_ge(v_lo, t // 4 + 1)
                last = pe.matmul(ps[:, t // 4, t % 4 * P:(t % 4 + 1) * P], X[:, 1 + t * P:1 + (t + 1) * P],
                                 w[:, 2, :], start=True, stop=True)
                if t % 4 == 3:
                    last.then_inc(p_v, 1)


def ring_slots():
    slots, n = {}, 0
    for w in range(-LEAD, GH * TILES):
        if w + LEAD < GH * TILES:
            for c in range(4):
                slots["scores", w + LEAD, c] = n
                n += 1
        h = w // TILES
        if h >= 1 and w % TILES == PVLAG:
            slots["output", h - 1] = n
            n += 1
        if -1 <= h < GH - 1 and w % TILES == MAXSTEP:
            slots["maxima", h + 1] = n
            n += 1
    slots["output", GH - 1] = n
    return slots


def stage_b(nc, scratch, max_scratch, ident, vtok, otok, qs, ks, small, sources):
    WARM = 20
    TOTAL = GH * TILES
    with ExitStack() as ctx:
        def sb(name, shape, dt=F32):
            return ctx.enter_context(nc.sbuf_tensor(name, shape, dt))

        def pb(name, shape):
            return ctx.enter_context(nc.psum_tensor(name, shape, F32))

        def sem(name):
            return ctx.enter_context(nc.semaphore(name))

        zero2 = sb("zero2", [2, SEQ], F32R)
        vs = sb("vs", [P, 2, TILES, VCOL])
        prob = sb("prob", [P, PSLOTS, SEQ])
        part = sb("part", [P, 2, TILES, 4])
        nmax = sb("nmax", [P, TILES])
        nmax_hi = sb("nmax_hi", [TILES, P], F32R)
        nmax_lo = sb("nmax_lo", [TILES, P], F32R)
        oacc = sb("oacc", [P, BANK])
        rden = sb("rden", [P, 4, 4])
        ps_ring = pb("ps_ring", [P, RING, BANK])
        ps_exp = pb("ps_exp", [P, 2, 2 * BANK])
        ps_o = pb("ps_o", [P, BANK])

        loaded = [sem(f"loaded{b}") for b in range(GBUF)]
        max_out, max_rows = sem("max_out"), sem("max_rows")
        g_init, g_vs, par = sem("g_init"), sem("g_vs"), sem("par")
        p_max, v_ring, v_nmax, p_maxt, v_mhi = (
            sem(n) for n in ("p_max", "v_ring", "v_nmax", "p_maxt", "v_mhi"))
        p_exp, a_exp, p_pv, a_oacc, p_ot, v_rden = (
            sem(n) for n in ("p_exp", "a_exp", "p_pv", "a_oacc", "p_otr", "v_rdenB"))
        slots = ring_slots()
        LOADS = 9

        block = ctx.enter_context(nc.Block())

        def walk(eng, step):
            for w in range(WARM):
                step(w, w, 0)
            with eng.Fori(0, 3) as g:
                for k in range(WARM, WARM + 4 * TILES):
                    step(g * (4 * TILES) + k, k, g)
            for w in range(WARM + 12 * TILES, TOTAL):
                step(w, w, 0)

        @block.sync
        def _(sp):
            def load(h, b):
                rows = bass.ds(h * GD, GD)
                for r, (qn, kn) in enumerate(((0, 2), (0, 3), (1, 2), (1, 3))):
                    sp.dma_start(qs[r * GD:(r + 1) * GD, b, :].bitcast(F32), scratch[qn, rows, :]).then_inc(loaded[b], 16)
                    sp.dma_start(ks[r * GD:(r + 1) * GD, b, :].bitcast(F32), scratch[kn, rows, :]).then_inc(loaded[b], 16)
                sp.dma_start(qs[SPLIT:SPLIT + 2, b, :].bitcast(F32), zero2[:].bitcast(F32)).then_inc(loaded[b], 16)

            def put_max(h, b, used):
                sp.wait_ge(v_ring, used)
                for r, src in ((0, nmax_hi), (1, nmax_lo)):
                    sp.dma_start(max_scratch[r], src[:].bitcast(F32)).then_inc(max_out, 16)
                sp.wait_ge(max_out, h * 32 + 32)
                sp.dma_start(qs[SPLIT:SPLIT + 2, b, :].bitcast(F32),
                             max_scratch.rearrange("r t q -> r (t q)")).then_inc(max_rows, 16)

            sp.wait_ge(g_init, 1)
            for h in range(GBUF):
                load(h, h)
            put_max(0, 0, slots["maxima", 0] + 1)

            def head(h, k, lead):
                put_max(h, k % GBUF, lead * ROUND + (slots["maxima", k] + 1))
                sp.wait_ge(p_exp, 2 * TILES * h)
                sp.wait_ge(p_pv, TILES * (h - 1) + 1) if k > 1 else None
                load(h + GBUF - 1, (k - 1) % GBUF)

            with sp.Fori(0, 3) as g:
                for k in range(1, 5):
                    head(g * 4 + k, k, g)
            for h in range(13, GH):
                put_max(h, h % GBUF, slots["maxima", h] + 1)
            sp.wait_ge(max_rows, 16 * GH)

        @block.gpsimd
        def _(pool):
            pool.memset(zero2[:].bitcast(F32), 0.0).then_inc(g_init, 1)
            pool.memset(vs[:], 0.0).then_inc(g_init, 1)
            pool.wait_ge(g_init, 2)
            pool.memset(vs[:, :, :, GD:GD + 1], 1.0).then_inc(g_init, 1)
            pool.wait_ge(g_init, 3)

            def values(h, b):
                pool.tensor_copy(vs[:, b, :, 0:GD], vtok[:, :, bass.ds(h * GD, GD)]).then_inc(g_vs, 1)

            values(0, 0)
            values(1, 1)

            lqs, lks, lg, lb, lb1, lb2, rope, carry_scale, mask = sources
            pool.memset(small["b1col"][:], 0.0).then_inc(g_init, 1)
            pool.wait_ge(g_init, 4)
            for k, vec in ((0, lqs), (2, lks)):
                rows, half = vec.rearrange("(o l) d -> o l d", o=1), HD // 2
                pool.dma_start(small["scales"][:, k], rows.broadcast_to([P, DEPTH, HD])).then_inc(par, 16)
                for a, b in ((0, half), (half, 0)):
                    pool.dma_start(small["scales"][:, k + 1, :, a:a + half],
                                   rows[:, :, b:b + half].broadcast_to([P, DEPTH, half])).then_inc(par, 16)
            for l in range(DEPTH):
                for name, vec in (("gcol", lg), ("bcol", lb), ("b2col", lb2)):
                    pool.dma_start(small[name][:, l:l + 1], vec[l].rearrange("(d o) -> d o", o=1)).then_inc(par, 16)
                for a in range(2):
                    for j in range(FFT):
                        rows = P if j < FFT - 1 else FFL
                        src = lb1[l, a * FF + j * P:a * FF + j * P + rows].rearrange("(d o) -> d o", o=1)
                        pool.dma_start(small["b1col"][0:rows, a, j, l:l + 1], src).then_inc(par, 16)
            for name, src in (("rope_sb", rope), ("cscale", carry_scale), ("mask_f", mask)):
                pool.dma_start(small[name][:], src).then_inc(par, 16)
            pool.wait_ge(par, 16 * (9 + 9 * DEPTH))
            with pool.Fori(1, GH // 2) as hh:
                for b in range(2):
                    pool.wait_ge(p_pv, TILES * (hh * 2 + b - 1))
                    values(hh * 2 + b, b)

        @block.vector
        def _(dve):
            def reduce_tile(u, ku, lead):
                t, b = ku % TILES, ku // TILES % 2
                for c in range(4):
                    dve.wait_ge(p_max, u * 4 + c + 1)
                    dve.tensor_reduce(part[:, b, t, c:c + 1], ps_ring[:, slots["scores", ku, c] % RING, :], AX.X,
                                      ALU.max).then_inc(v_ring, 1)
                if t == TILES - 1:
                    dve.wait_ge(v_ring, lead * ROUND + (slots["scores", ku, 3] + 1))
                    if ku >= TILES:
                        dve.wait_ge(p_maxt, (u - (TILES - 1)) // TILES)
                    dve.tensor_reduce(nmax[:], part[:, b], AX.X, ALU.max, negate=True).then_inc(v_nmax, 1)

            def split_max(h, kh):
                src = ps_ring[0:TILES, slots["maxima", kh] % RING, 0:P]
                dve.wait_ge(p_maxt, h + 1)
                if kh > 0:
                    dve.wait_ge(max_rows, h * 16)
                dve.tensor_copy(nmax_hi[:], src).then_inc(v_mhi, 1)
                dve.wait_ge(v_mhi, h + 1)
                dve.tensor_tensor(nmax_lo[:], src, nmax_hi[:].bitcast(F32), ALU.subtract).then_inc(v_ring, 1)

            def finish_head(h, kh):
                dve.wait_ge(p_ot, h + 1)
                if kh == GH - 1:
                    dve.wait_ge(v_ring, slots["output", kh])
                o = ps_ring[:, slots["output", kh] % RING, :].rearrange("p (s c m) -> p c s m", s=4, c=4)
                dve.reciprocal(rden[:], o[:, :, :, GD]).then_inc(v_rden, 1)
                dve.wait_ge(v_rden, h + 1)
                dve.tensor_tensor(otok[:, :, bass.ds(h * GD, GD)].rearrange("p (c s) d -> p c s d", c=4),
                                  o[:, :, :, 0:GD], rden[:].unsqueeze(3).broadcast_to([P, 4, 4, GD]),
                                  ALU.mult).then_inc(v_ring, 1)

            for u in range(LEAD):
                reduce_tile(u, u, 0)
                if u - LEAD == MAXSTEP - TILES:
                    split_max(0, 0)

            def step(w, k, lead):
                if not (isinstance(w, int) and w + LEAD >= TOTAL):
                    reduce_tile(w + LEAD, k + LEAD, lead)
                if k % TILES == PVLAG and k > PVLAG:
                    finish_head(lead * 4 + (k // TILES - 1), k // TILES - 1)
                if k % TILES == MAXSTEP and k < TOTAL - TILES:
                    split_max(lead * 4 + (k // TILES + 1), k // TILES + 1)

            walk(dve, step)
            finish_head(GH - 1, GH - 1)

        @block.scalar
        def _(act):
            def step(w, k, lead):
                for half in range(2):
                    act.wait_ge(p_exp, w * 2 + half + 1)
                    if k >= PSLOTS:
                        act.wait_ge(p_pv, lead * (4 * TILES) + (k - PSLOTS + 1))
                    act.activation(prob[:, k % PSLOTS, half * 2 * BANK:(half + 1) * 2 * BANK],
                                   ps_exp[:, half, :], ACT.Exp, scale=GD ** -0.5).then_inc(a_exp, 1)
                if k % TILES == 1 and k > 1:
                    save_o(lead * 4 + (k // TILES - 1), k > TILES + 1)

            def save_o(h, later):
                act.wait_ge(p_pv, (h + 1) * TILES)
                if later:
                    act.wait_ge(p_ot, h)
                act.activation(oacc[:], ps_o[:], ACT.Copy).then_inc(a_oacc, 1)

            walk(act, step)
            save_o(GH - 1, True)

        @block.tensor
        def _(pe):
            def free_slot(n, lead):
                if n >= RING:
                    pe.wait_ge(v_ring, lead * ROUND + (n - RING + 1))
                return n % RING

            def max_scores(u, ku, c, lead):
                b, t = ku // TILES % GBUF, ku % TILES
                if t == 0 and c == 0:
                    pe.wait_ge(loaded[b], ((u - ku % (GBUF * TILES)) // (GBUF * TILES) + 1) * (LOADS * 16))
                r = free_slot(slots["scores", ku, c], lead)
                pe.matmul(ps_ring[:, r, :], qs[:, b, t * P:(t + 1) * P], ks[:, b, c * BANK:(c + 1) * BANK],
                          start=True, stop=True).then_inc(p_max, 1)

            def turn_max(h, kh, lead):
                pe.wait_ge(v_nmax, h + 1)
                r = free_slot(slots["maxima", kh], lead)
                pe.transpose(ps_ring[0:TILES, r, 0:P], nmax[:], ident[:]).then_inc(p_maxt, 1)

            def turn_o(h, kh, lead):
                pe.wait_ge(a_oacc, h + 1)
                r = free_slot(slots["output", kh], lead)
                for s in range(4):
                    last = pe.transpose(ps_ring[:, r, s * P:(s + 1) * P], oacc[:, s * P:(s + 1) * P], ident[:])
                last.then_inc(p_ot, 1)

            def exp_scores(w, k, half):
                b, t = k // TILES % GBUF, k % TILES
                if t == 0 and half == 0:
                    pe.wait_ge(max_rows, (w // TILES + 1) * 16)
                if k > 0:
                    pe.wait_ge(a_exp, w * 2 + half - 1)
                for cc in range(2):
                    last = pe.matmul(ps_exp[:, half, cc * BANK:(cc + 1) * BANK], ks[:, b, t * P:(t + 1) * P],
                                     qs[:, b, (2 * half + cc) * BANK:(2 * half + cc + 1) * BANK],
                                     start=True, stop=True)
                last.then_inc(p_exp, 1)

            def value_products(w, k):
                kk = k - PVLAG
                h, t = kk // TILES, kk % TILES
                if t == 0:
                    pe.wait_ge(g_vs, (w - PVLAG) // TILES + 1)
                    if kk >= TILES:
                        pe.wait_ge(a_oacc, (w - PVLAG) // TILES)
                pe.wait_ge(a_exp, (w - PVLAG) * 2 + 2)
                for c in range(4):
                    last = pe.matmul(ps_o[32 * c:32 * c + VCOL, :], vs[:, h % 2, t, :],
                                     prob[:, kk % PSLOTS, c * BANK:(c + 1) * BANK],
                                     start=(t == 0), stop=(t == TILES - 1), skip_group_check=True)
                last.then_inc(p_pv, 1)

            for u in range(LEAD):
                for c in range(4):
                    max_scores(u, u, c, 0)
                if u - LEAD == MAXSTEP - TILES:
                    turn_max(0, 0, 0)

            def step(w, k, lead):
                ahead = not (isinstance(w, int) and w + LEAD >= TOTAL)
                if ahead:
                    max_scores(w + LEAD, k + LEAD, 0, lead)
                    max_scores(w + LEAD, k + LEAD, 1, lead)
                exp_scores(w, k, 0)
                exp_scores(w, k, 1)
                if ahead:
                    max_scores(w + LEAD, k + LEAD, 2, lead)
                    max_scores(w + LEAD, k + LEAD, 3, lead)
                if k >= PVLAG:
                    value_products(w, k)
                if k % TILES == PVLAG and k > PVLAG:
                    turn_o(lead * 4 + (k // TILES - 1), k // TILES - 1, lead)
                if k % TILES == MAXSTEP and k < TOTAL - TILES:
                    turn_max(lead * 4 + (k // TILES + 1), k // TILES + 1, lead)

            walk(pe, step)
            for w in range(TOTAL, TOTAL + PVLAG):
                value_products(w, w)
            turn_o(GH - 1, GH - 1, 0)


def stage_c(nc, ident, otok, wout, bout, att_scratch):
    with ExitStack() as ctx:
        def sem(name):
            return ctx.enter_context(nc.semaphore(name))

        ot = ctx.enter_context(nc.sbuf_tensor("ot", [P, SEQ], F32))
        att = ctx.enter_context(nc.sbuf_tensor("att", [P, SEQ], F32))
        ps = ctx.enter_context(nc.psum_tensor("psC", [P, 8, BANK], F32))
        p_t, a_t, p_w, v_w, stored = sem("p_t"), sem("a_t"), sem("p_w"), sem("v_w"), sem("storedC")
        block = ctx.enter_context(nc.Block())

        @block.sync
        def _(sp):
            for c in range(4):
                cols = slice(c * BANK, (c + 1) * BANK)
                sp.wait_ge(v_w, c + 1)
                sp.dma_start(att_scratch[:, cols], att[:, cols]).then_inc(stored, 16)
            sp.wait_ge(stored, 64)

        @block.tensor
        def _(pe):
            for t in range(TILES):
                last = pe.transpose(ps[:, t // 4, t % 4 * P:(t % 4 + 1) * P], otok[:, t, :], ident[:])
                if t % 4 == 3:
                    last.then_inc(p_t, 1)
            for c in range(4):
                pe.wait_ge(a_t, c + 1)
                pe.matmul(ps[:, 4 + c, :], wout[:], ot[:, c * BANK:(c + 1) * BANK],
                          start=True, stop=True).then_inc(p_w, 1)

        @block.scalar
        def _(act):
            for c in range(4):
                act.wait_ge(p_t, c + 1)
                act.activation(ot[:, c * BANK:(c + 1) * BANK], ps[:, c, :], ACT.Copy).then_inc(a_t, 1)

        @block.vector
        def _(dve):
            for c in range(4):
                dve.wait_ge(p_w, c + 1)
                dve.tensor_scalar(att[:, c * BANK:(c + 1) * BANK], ps[:, 4 + c, :], bout[:, 0:1], None,
                                  ALU.add).then_inc(v_w, 1)


def stage_d(nc, lqkv, lwo, lw1, lw2, small_params, ident, X):
    with ExitStack() as ctx:
        def sb(name, shape, dt=F32):
            return ctx.enter_context(nc.sbuf_tensor(name, shape, dt))

        def sem(name):
            return ctx.enter_context(nc.semaphore(name))

        w_hi = sb("w_hi", [P, 2, 3 * INNER], F32R)
        w_lo = sb("w_lo", [P, 2, 3 * INNER], F32R)
        w_new = sb("w_new", [P, 4, 3, HD])
        wo_sb = sb("wo_sb", [P, PAIRS, DIM])
        w1_sb = sb("w1_sb", [P, 2, FFT * P])
        w2_sb = sb("w2_sb", [P, FFT, DIM])
        scales, gcol, bcol, b2col, b1col, rope_sb, cscale, mask_f = (small_params[n] for n in (
            "scales", "gcol", "bcol", "b2col", "b1col", "rope_sb", "cscale", "mask_f"))
        mask_b = sb("mask_b", [P, 2, KEYS], BF16)
        ident_b = sb("ident_b", [P, P], BF16)
        mean_w = sb("mean_w", [P, P])
        eps = sb("eps", [P, 1])
        Y = sb("Y", [P, 1 + SEQ])
        xs = sb("xs", [P, P])
        xs_hi = sb("xs_hi", [P, P], F32R)
        xs_lo = sb("xs_lo", [P, P], F32R)
        ys = sb("ys", [P, P])
        tab = sb("tab", [P, 4, HD])
        rot = sb("rot", [P, 2, INNER])
        rot2 = sb("rot2", [P, 2, INNER])
        rotn = sb("rotn", [P, 2, INNER])
        sq = sb("sqD", [P, 2, INNER])
        ssum = sb("ssum", [P, 2, NH])
        clamped = sb("clamped", [P, 2, NH])
        lognorm = sb("lognorm", [P, 2, NH])
        rnorm = sb("rnorm", [P, 2, NH])
        qT = sb("qT", [P, PAIRS, P])
        kT = sb("kT", [P, PAIRS, 2, WIN + P])
        vtile = sb("vtile", [P, 4, INNER])
        vwin = sb("vwin", [P, NWIN, 2, PAIRS, HD])
        mx = sb("mx", [P, NH])
        prob = sb("probD", [P, NH * KEYS])
        den = sb("den", [P, NH])
        rden = sb("rdenD", [P, NH])
        pT = sb("pT", [P, PAIRS, P])
        on = sb("on", [P, INNER])
        oT = sb("oT", [P, PAIRS, P])
        yc = sb("yc", [P, P])
        ysq = sb("ysq", [P, P])
        logvar = sb("logvar", [P, P])
        rstd = sb("rstdD", [P, P])
        yn = sb("yn", [P, P])
        gate = sb("gate", [P, FFT, P])
        big = [ctx.enter_context(nc.psum_tensor(f"big{n}", [P, 2 * BANK], F32)) for n in range(3)]
        small = [ctx.enter_context(nc.psum_tensor(f"small{n}", [P, BANK], F32)) for n in range(2)]

        w_qkv, w_o, w_1, w_2, vmoved = sem("w_qkv"), sem("w_o"), sem("w_1"), sem("w_2"), sem("vmoved")
        g_memset, v_memset, v_cst = sem("g_memset"), sem("v_memset"), sem("v_cst")
        (p_tq, p_tk, p_ot, p_q, p_mu, p_k, p_wo, p_v, p_var, p_pt, p_gate, p_a, p_s, p_pv, p_w2) = (
            sem(f"p_{n}") for n in ("tq", "tk", "otD", "q", "mu", "k", "wo", "vD", "var", "pt", "gate", "a", "s",
                                    "pvD", "w2"))
        (a_carry, a_qT, a_kT, a_oT, a_sqq, a_sqk, a_v, a_lnn, a_lnv, a_rnorm, a_rstd, a_pT, a_gelu, a_exp) = (
            sem(f"a_{n}") for n in ("carry", "qT", "kT", "oT", "sqq", "sqk", "vD", "lnn", "lnv", "rnorm", "rstdD", "pT", "gelu", "expD"))
        (v_q, v_yc, v_ysq, v_ssq, v_k, v_ssk, v_clamp, v_y, v_xhi, v_whi, v_yn0, v_yn, v_hid, v_max, v_sub,
         v_on, v_den, v_rden, v_x) = (
            sem(f"v_{n}") for n in ("q", "yc", "ysq", "ssq", "k", "ssk", "clamp", "y", "xhi", "whi", "yn0",
                                    "yn", "hid", "max", "sub", "on", "den", "rdenD", "x"))
        (g_addq, g_mulq, g_addk, g_mulk, g_xs, g_xlo, g_wlo, g_tab, g_ys) = (
            sem(f"g_{n}") for n in ("addq", "mulq", "addk", "mulk", "xs", "xlo", "wlo", "tab", "ys"))

        block = ctx.enter_context(nc.Block())
        NFIRST, NSHARE, NO, N1, N2, NVM = 5, 2, 2, 2, FFT, 10

        def pipeline(eng, step):
            for i in range(LAST):
                step(i)
            for ends in ((LAST, STEPS - TILES), (STEPS - TILES, STEPS)):
                with eng.Fori(*ends) as i:
                    step(i, ends[1] < STEPS)
            for i in range(STEPS, STEPS + LAST):
                step(i, False)

        def share(w, l, t):
            w = w[:, bass.ds(l & 1, 1), :].rearrange("f o (a t d) -> f (o a) t d", a=3, d=HD)
            return w[:, :, bass.ds(t, 1), :].rearrange("f a o d -> f a (o d)")

        def on_tile(i, lag):
            n = i - lag
            return None if isinstance(n, int) and not 0 <= n < STEPS else n

        def upto(value):
            return min(value, STEPS) if isinstance(value, int) else value

        @block.sync
        def _(sp):
            def load_first():
                for part in range(2):
                    src = lqkv[0, :, part * INNER:(part + 1) * INNER].rearrange("f (s p d) -> f s p d", s=2, d=HD)
                    dst = rot[:, part].rearrange("f (p s d) -> f s p d", s=2, d=HD)
                    for s in range(2):
                        sp.dma_start(dst[:, s], src[:, s]).then_inc(w_qkv, 16)
                sp.dma_start(rotn[:, 0], lqkv[0, :, 2 * INNER:]).then_inc(w_qkv, 16)

            def load_o(l):
                src = lwo[l].rearrange("(s p d) n -> s d p n", s=2, d=HD)
                for s in range(2):
                    sp.dma_start(wo_sb[s * HD:(s + 1) * HD], src[s]).then_inc(w_o, 16)

            def load_1(l):
                for a in range(2):
                    sp.dma_start(w1_sb[:, a, 0:FF], lw1[l, :, a * FF:(a + 1) * FF]).then_inc(w_1, 16)

            def load_2(l):
                for j in range(FFT):
                    rows = P if j < FFT - 1 else FFL
                    sp.dma_start(w2_sb[0:rows, j, :], lw2[l, j * P:j * P + rows, :]).then_inc(w_2, 16)

            def move_v(n, r, first=False):
                if first:
                    sp.wait_ge(a_v, n + 1)
                else:
                    sp.wait_ge(p_pv, n)
                sp.wait_ge(g_memset, 2)
                old = (r + 3) & 3
                cur, prev = vtile[:, r:r + 1, :], vtile[:, old:old + 1, :]
                for s in range(2):
                    half = slice(s * PAIRS * HD, (s + 1) * PAIRS * HD)
                    row = s * KEYS
                    dst = vwin[:].rearrange("p c s q d -> p c s (q d)")
                    sp.dma_start(dst[row:row + WIN, 0:1, s, :], prev[P - WIN:P, :, half]).then_inc(vmoved, 16)
                    sp.dma_start(dst[row + WIN:row + KEYS, 0:1, s, :], cur[0:WIN, :, half]).then_inc(vmoved, 16)
                    for c in range(1, NWIN):
                        sp.dma_start(dst[row:row + KEYS, c:c + 1, s, :],
                                     cur[WIN * (c - 1):WIN * (c + 1), :, half]).then_inc(vmoved, 16)

            def layer(l):
                for t in (-1, 0):
                    move_v(l * TILES + t, t & 3)
                sp.wait_ge(p_wo, l * TILES)
                load_o(l)
                move_v(l * TILES + 1, 1)
                sp.wait_ge(p_a, l * TILES)
                load_1(l)
                move_v(l * TILES + 2, 2)
                sp.wait_ge(p_w2, l * TILES)
                load_2(l)
                with sp.Fori(0, 3) as g:
                    for t in range(3, 7):
                        move_v(l * TILES + g * 4 + t, t & 3)

            load_first()
            load_o(0)
            sp.wait_ge(v_memset, 2)
            load_1(0)
            load_2(0)
            move_v(0, 0, first=True)
            for t in (1, 2):
                move_v(t, t & 3)
            with sp.Fori(0, 3) as g:
                for t in range(3, 7):
                    move_v(g * 4 + t, t & 3)
            with sp.Fori(1, DEPTH) as l:
                layer(l)
            move_v(STEPS - 1, 3)
            sp.wait_ge(vmoved, NVM * 16 * STEPS)

        @block.gpsimd
        def _(pool):
            pool.memset(vwin[:], 0.0).then_inc(g_memset, 1)
            pool.memset(vtile[:, 3, :], 0.0).then_inc(g_memset, 1)
            pool.memset(Y[:, 0:1], 0.0).then_inc(g_memset, 1)

            def shift(dst, src, t, before, done, n):
                at = t * P
                pool.tensor_copy(dst[0:P // 2, :], src[0:P // 2, bass.ds(at + 1, P)])
                for s_before, value in before:
                    need(pool, s_before, value)
                pool.tensor_copy(dst[P // 2:P, :], src[P // 2:P, bass.ds(at, P)]).then_inc(done, 1)
                pool.wait_ge(done, n + 1)

            def prepare(n, before):
                t, l = n & (TILES - 1), layer_of(n)
                need(pool, g_xlo, n)
                shift(xs, X, t, before, g_xs, n)
                need(pool, v_k, n)
                src = rope_sb[:, bass.ds(t, 1), :, :].rearrange("p o k d -> p (o k) d")
                fac = scales[:, :, bass.ds(l, 1), :].rearrange("p k o d -> p (k o) d")
                pool.tensor_tensor(tab[:], src, fac, ALU.mult).then_inc(g_tab, 1)
                pool.wait_ge(v_xhi, n + 1)
                need(pool, p_v, n)
                pool.tensor_tensor(xs_lo[:], xs[:], xs_hi[:].bitcast(F32), ALU.subtract).then_inc(g_xlo, 1)

            def step(i, split=True):
                if (n := on_tile(i, 0)) is not None:
                    for part, (done, add) in enumerate(((v_q, g_addq), (v_k, g_addk))):
                        pool.wait_ge(done, n + 1)
                        pool.tensor_tensor(rot[:, part], rot[:, part], rot2[:, part], ALU.add).then_inc(add, 1)
                if (n := on_tile(i, -1)) is not None:
                    prepare(n, [(g_addk, n)])
                if (n := on_tile(i, 0)) is not None:
                    pool.wait_ge(a_rnorm, n + 1)
                    for part, (add, turned, mul) in enumerate(((g_addq, p_tq, g_mulq), (g_addk, p_tk, g_mulk))):
                        pool.wait_ge(add, n + 1)
                        need(pool, turned, n)
                        pool.tensor_tensor(rotn[:, part].rearrange("p (h d) -> p h d", d=HD),
                                           rot[:, part].rearrange("p (h d) -> p h d", d=HD),
                                           rnorm[:, part].unsqueeze(2).broadcast_to([P, NH, HD]),
                                           ALU.mult).then_inc(mul, 1)
                if (n := on_tile(i, 3)) is not None:
                    pool.wait_ge(v_y, n + 1)
                    need(pool, v_yc, n)
                    shift(ys, Y, n & (TILES - 1), [(g_mulk, upto(i + 1))], g_ys, n)
                if split and (n := on_tile(i, 0)) is not None:
                    pool.wait_ge(v_whi, TILES + n + 1)
                    l, t = layer_of(n) + 1, n & (TILES - 1)
                    pool.tensor_tensor(share(w_lo, l, t), w_new[:, bass.ds(n & 3, 1)].rearrange("f o a d -> f (o a) d"),
                                       share(w_hi, l, t).bitcast(F32), ALU.subtract).then_inc(g_wlo, 1)

            prepare(0, [(g_memset, 3)])
            pool.wait_ge(v_whi, TILES)
            pool.tensor_tensor(w_lo[:, 0, 0:2 * INNER], rot[:].rearrange("p a d -> p (a d)"),
                               w_hi[:, 0, 0:2 * INNER].bitcast(F32), ALU.subtract)
            pool.tensor_tensor(w_lo[:, 0, 2 * INNER:], rotn[:, 0], w_hi[:, 0, 2 * INNER:].bitcast(F32),
                               ALU.subtract).then_inc(g_wlo, TILES)
            for i in range(LAST):
                step(i)
            with pool.Fori(LAST, STEPS - TILES) as i:
                step(i)
            with pool.Fori(STEPS - TILES, STEPS - 1) as i:
                step(i, False)
            for i in range(STEPS - 1, STEPS + LAST):
                step(i, False)

        @block.vector
        def _(dve):
            dve.memset(w1_sb[:], 0.0).then_inc(v_memset, 1)
            dve.memset(w2_sb[:], 0.0).then_inc(v_memset, 1)
            dve.memset(eps[:], EPS)
            dve.memset(kT[:], 0.0).then_inc(v_memset, 1)
            dve.memset(mean_w[:], 1.0 / DIM).then_inc(v_memset, 1)
            dve.tensor_copy(mask_b[:], mask_f[:]).then_inc(v_cst, 1)
            dve.tensor_copy(ident_b[:], ident[:]).then_inc(v_cst, 1)
            dve.wait_ge(g_memset, 3)

            def rotate(part, ps):
                x3 = ps[:].rearrange("p (h d) -> p h d", d=HD)
                r1 = rot[:, part].rearrange("p (h d) -> p h d", d=HD)
                r2 = rot2[:, part].rearrange("p (h d) -> p h d", d=HD)
                half = HD // 2
                dve.tensor_tensor(r1, x3, tab[:, 2 * part].unsqueeze(1).broadcast_to([P, NH, HD]), ALU.mult)
                for a, b in ((0, half), (half, 0)):
                    last = dve.tensor_tensor(r2[:, :, a:a + half], x3[:, :, b:b + half],
                                             tab[:, 2 * part + 1, a:a + half].unsqueeze(1)
                                             .broadcast_to([P, NH, half]), ALU.mult)
                return last

            def sum_squares(part, n, squares, s_sum):
                dve.wait_ge(squares, n + 1)
                dve.tensor_reduce(ssum[:, part], sq[:, part].rearrange("p (h d) -> p h d", d=HD), AX.X,
                                  ALU.add).then_inc(s_sum, 1)

            def split_x(n):
                dve.wait_ge(g_xs, n + 1)
                need(dve, p_v, n)
                dve.tensor_copy(xs_hi[:], xs[:]).then_inc(v_xhi, 1)

            dve.wait_ge(w_qkv, NFIRST * 16)
            dve.tensor_copy(w_hi[:, 0, 0:2 * INNER], rot[:].rearrange("p a d -> p (a d)"))
            dve.tensor_copy(w_hi[:, 0, 2 * INNER:], rotn[:, 0]).then_inc(v_whi, TILES)
            split_x(0)

            def step(i, split=True):
                if (n := on_tile(i, 2)) is not None:
                    dve.wait_ge(a_exp, n + 1)
                    dve.tensor_reduce(den[:], prob[:].rearrange("p (h k) -> p h k", k=KEYS), AX.X,
                                      ALU.add).then_inc(v_den, 1)
                    dve.wait_ge(v_den, n + 1)
                    dve.reciprocal(rden[:], den[:]).then_inc(v_rden, 1)
                if (n := on_tile(i, 0)) is not None:
                    dve.wait_ge(a_sqq, n + 1)
                    dve.wait_ge(g_tab, n + 1)
                    need(dve, g_mulq, n)
                    rotate(0, big[0]).then_inc(v_q, 1)
                if (n := on_tile(i, 4)) is not None:
                    dve.wait_ge(p_mu, n + 1)
                    dve.tensor_tensor(yc[:], ys[:], small[1][:, 0:P], ALU.subtract).then_inc(v_yc, 1)
                    dve.wait_ge(v_yc, n + 1)
                    need(dve, p_var, n)
                    dve.tensor_tensor(ysq[:], yc[:], yc[:], ALU.mult).then_inc(v_ysq, 1)
                if (n := on_tile(i, 5)) is not None:
                    l = layer_of(n)
                    dve.wait_ge(p_w2, n + 1)
                    cols = bass.ds((n & (TILES - 1)) * P + 1, P)
                    dve.scalar_tensor_tensor(out=X[:, cols], in0=small[0][:, 0:P], scalar=b2col[:, bass.ds(l, 1)],
                                             in1=Y[:, cols], op0=ALU.add, op1=ALU.add).then_inc(v_x, 1)
                if (n := on_tile(i, 0)) is not None:
                    dve.wait_ge(a_sqk, n + 1)
                    need(dve, g_mulk, n)
                    rotate(1, big[1]).then_inc(v_k, 1)
                    sum_squares(0, n, a_sqq, v_ssq)
                    sum_squares(1, n, a_sqk, v_ssk)
                    dve.wait_ge(v_ssk, n + 1)
                    need(dve, a_lnn, n)
                    dve.tensor_scalar(clamped[:], ssum[:], 1e-24, None, ALU.max).then_inc(v_clamp, 1)
                if (n := on_tile(i, 3)) is not None:
                    dve.wait_ge(p_wo, n + 1)
                    cols = bass.ds((n & (TILES - 1)) * P + 1, P)
                    dve.tensor_tensor(Y[:, cols], small[0][:, 0:P], X[:, cols], ALU.add).then_inc(v_y, 1)
                if (n := on_tile(i, 4)) is not None:
                    l = layer_of(n)
                    dve.wait_ge(a_rstd, n + 1)
                    dve.tensor_tensor(ysq[:], yc[:], rstd[:], ALU.mult).then_inc(v_yn0, 1)
                    dve.wait_ge(v_yn0, n + 1)
                    need(dve, p_a, n)
                    dve.tensor_scalar(yn[:], ysq[:], gcol[:, bass.ds(l, 1)], bcol[:, bass.ds(l, 1)], ALU.mult,
                                      ALU.add).then_inc(v_yn, 1)
                if (n := on_tile(i, -1)) is not None:
                    split_x(n)
                if (n := on_tile(i, 1)) is not None:
                    s3 = big[1][:].rearrange("p (h k) -> p h k", k=KEYS)
                    dve.wait_ge(p_s, n + 1)
                    dve.tensor_reduce(mx[:], s3, AX.X, ALU.max).then_inc(v_max, 1)
                    dve.wait_ge(v_max, n + 1)
                    need(dve, p_pt, n)
                    dve.tensor_tensor(prob[:].rearrange("p (h k) -> p h k", k=KEYS), s3,
                                      mx[:].unsqueeze(2).broadcast_to([P, NH, KEYS]), ALU.subtract)\
                       .then_inc(v_sub, 1)
                if split and (n := on_tile(i, 0)) is not None:
                    l, t = layer_of(n) + 1, n & (TILES - 1)
                    dve.wait_ge(w_qkv, (n + 1) * (NSHARE * 16) + NFIRST * 16)
                    dve.tensor_copy(share(w_hi, l, t), w_new[:, bass.ds(n & 3, 1)].rearrange(
                        "f o a d -> f (o a) d")).then_inc(v_whi, 1)
                if (n := on_tile(i, 4)) is not None:
                    l = layer_of(n)
                    dve.wait_ge(p_a, n + 1)
                    dve.wait_ge(a_gelu, n + 1)
                    need(dve, p_w2, n)
                    for j in range(FFT):
                        last = dve.scalar_tensor_tensor(
                            out=gate[:, j, :], in0=small[0][:, j * P:(j + 1) * P],
                            scalar=b1col[:, 0, j, bass.ds(l, 1)], in1=gate[:, j, :], op0=ALU.add, op1=ALU.mult)
                    last.then_inc(v_hid, 1)
                if (n := on_tile(i, 2)) is not None:
                    dve.wait_ge(p_pv, n + 1)
                    dve.wait_ge(v_rden, n + 1)
                    need(dve, p_ot, n)
                    dve.tensor_tensor(on[:].rearrange("p (h d) -> p h d", d=HD),
                                      big[2][:].rearrange("p (h d) -> p h d", d=HD),
                                      rden[:].unsqueeze(2).broadcast_to([P, NH, HD]), ALU.mult).then_inc(v_on, 1)

            for i in range(LAST):
                step(i)
            with dve.Fori(LAST, STEPS - TILES) as i:
                step(i)
            with dve.Fori(STEPS - TILES, STEPS - 1) as i:
                step(i, False)
            for i in range(STEPS - 1, STEPS + LAST):
                step(i, False)
            dve.wait_ge(v_x, STEPS)

        @block.scalar
        def _(act):
            def load_share(c):
                l, t, r = (c >> 4) + 1, c & (TILES - 1), c & 3
                head = (t >> 1) + (t & 1) * PAIRS
                if not isinstance(c, int):
                    l = l.with_bounds(min_val=1, max_val=DEPTH - 1)
                    head = head.with_bounds(min_val=0, max_val=NH - 1)
                heads = lqkv[bass.ds(l, 1)].rearrange("o f (a h d) -> (o f) a h d", a=3, d=HD)
                for at, parts in ((head, slice(0, 2)), (t, slice(2, 3))):
                    dst = w_new[:, bass.ds(r, 1), parts].rearrange("f o a d -> f (o a) d")
                    src = heads[:, parts, bass.ds(at, 1), :].rearrange("f a o d -> f a (o d)")
                    act.dma_start(dst, src).then_inc(w_qkv, 16)

            act.wait_ge(v_memset, 3)
            act.wait_ge(w_qkv, NFIRST * 16)

            def copy(dst, src):
                return act.activation(dst, src, ACT.Copy)

            def step(i, split=True):
                if (n := on_tile(i, 0)) is not None:
                    act.wait_ge(p_q, n + 1)
                    need(act, v_ssq, n)
                    act.activation(sq[:, 0], big[0][:], ACT.Square).then_inc(a_sqq, 1)
                if (n := on_tile(i, 3)) is not None:
                    act.wait_ge(p_ot, n + 1)
                    need(act, p_wo, n)
                    copy(oT[:].rearrange("p q t -> p (q t)"), big[2][:]).then_inc(a_oT, 1)
                if (n := on_tile(i, 0)) is not None:
                    act.wait_ge(p_k, n + 1)
                    need(act, v_ssk, n)
                    act.activation(sq[:, 1], big[1][:], ACT.Square).then_inc(a_sqk, 1)
                if (n := on_tile(i, 1)) is not None:
                    act.wait_ge(p_tk, n + 1)
                    act.wait_ge(a_carry, n + 1)
                    for s in range(2):
                        rows = slice(s * HD, (s + 1) * HD)
                        last = copy(kT[rows, :, s, WIN:WIN + P], big[2][rows].rearrange("p (q t) -> p q t", t=P))
                    last.then_inc(a_kT, 1)
                if (n := on_tile(i, 0)) is not None:
                    act.wait_ge(p_v, n + 1)
                    need(act, vmoved, (n - 2) * (NVM * 16))
                    copy(vtile[:, bass.ds(n & 3, 1), :].rearrange("p o d -> p (o d)"), big[0][:]).then_inc(a_v, 1)
                if (n := on_tile(i, 1)) is not None:
                    act.wait_ge(p_tq, n + 1)
                    copy(qT[:].rearrange("p q t -> p (q t)"), big[2][:]).then_inc(a_qT, 1)
                if split and (n := on_tile(i, 0)) is not None:
                    need(act, v_whi, TILES + n)
                    load_share(n)
                if (n := on_tile(i, 0)) is not None:
                    act.wait_ge(v_clamp, n + 1)
                    act.activation(lognorm[:], clamped[:], ACT.Ln).then_inc(a_lnn, 1)
                if (n := on_tile(i, 4)) is not None:
                    act.wait_ge(p_var, n + 1)
                    act.activation(logvar[:], small[1][:, 0:P], ACT.Ln, bias=eps[:, 0:1]).then_inc(a_lnv, 1)
                if (n := on_tile(i, 0)) is not None:
                    act.wait_ge(a_lnn, n + 1)
                    need(act, g_mulk, n)
                    act.activation(rnorm[:], lognorm[:], ACT.Exp, scale=-0.5).then_inc(a_rnorm, 1)
                if (n := on_tile(i, 4)) is not None:
                    act.wait_ge(a_lnv, n + 1)
                    need(act, v_yn0, n)
                    act.activation(rstd[:], logvar[:], ACT.Exp, scale=-0.5).then_inc(a_rstd, 1)
                if (n := on_tile(i, 2)) is not None:
                    act.wait_ge(p_pt, n + 1)
                    need(act, p_pv, n)
                    copy(pT[:].rearrange("p q t -> p (q t)"), big[0][:]).then_inc(a_pT, 1)
                if (n := on_tile(i, 0)) is not None:
                    need(act, p_s, n)
                    need(act, a_kT, n)
                    act.activation(kT[:, :, :, 0:WIN], kT[:, :, :, P:P + WIN], ACT.Copy,
                                   scale=cscale[:, 0:1]).then_inc(a_carry, 1)
                if (n := on_tile(i, 4)) is not None:
                    act.wait_ge(p_gate, n + 1)
                    need(act, p_w2, n)
                    for j in range(FFT):
                        last = act.activation(gate[:, j, :], small[1][:, j * P:(j + 1) * P], ACT.Gelu,
                                              bias=b1col[:, 1, j, bass.ds(layer_of(n), 1)])
                    last.then_inc(a_gelu, 1)
                if (n := on_tile(i, 1)) is not None:
                    act.preload_act_table_set("natural_log_exp_and_others")
                    act.wait_ge(v_sub, n + 1)
                    act.activation(prob[:], prob[:], ACT.Exp).then_inc(a_exp, 1)

            pipeline(act, step)

        @block.tensor
        def _(pe):
            pe.wait_ge(v_memset, 4)
            pe.wait_ge(v_cst, 2)

            def turn(ps, src):
                for p in range(PAIRS):
                    last = pe.transpose(ps[:, p * P:(p + 1) * P], src[:, p * P:(p + 1) * P], ident[:])
                return last

            def project(ps, part, l):
                hi, lo = (w[:, bass.ds(l & 1, 1), :].rearrange("f o d -> f (o d)") for w in (w_hi, w_lo))
                for h in range(2):
                    at = part * INNER + h * BANK
                    for k, (a, b) in enumerate(((xs_hi, hi), (xs_hi, lo), (xs_lo, hi))):
                        last = pe.matmul(ps[:, h * BANK:(h + 1) * BANK], a[:], b[:, at:at + BANK],
                                         start=(k == 0), stop=(k == 2))
                return last

            def step(i, split=True):
                if (n := on_tile(i, 0)) is not None:
                    pe.wait_ge(g_xlo, n + 1)
                    pe.wait_ge(g_wlo, (layer_of(n) + 1) * TILES)
                    need(pe, a_v, n)
                    need(pe, a_pT, n - 2)
                    project(big[0], 0, layer_of(n)).then_inc(p_q, 1)
                if (n := on_tile(i, 4)) is not None:
                    pe.wait_ge(g_ys, n + 1)
                    need(pe, a_gelu, n)
                    pe.matmul(small[1][:, 0:P], mean_w[:], ys[:], start=True, stop=True).then_inc(p_mu, 1)
                if (n := on_tile(i, 3)) is not None:
                    pe.wait_ge(v_on, n + 1)
                    turn(big[2], on).then_inc(p_ot, 1)
                if (n := on_tile(i, 0)) is not None:
                    need(pe, v_sub, n - 1)
                    project(big[1], 1, layer_of(n)).then_inc(p_k, 1)
                if (n := on_tile(i, 1)) is not None:
                    pe.wait_ge(g_mulk, n + 1)
                    need(pe, a_oT, i - 2)
                    turn(big[2], rotn[:, 1]).then_inc(p_tk, 1)
                if (n := on_tile(i, 5)) is not None:
                    pe.wait_ge(v_hid, n + 1)
                    pe.wait_ge(w_2, (layer_of(n) + 1) * (N2 * 16))
                    for j in range(FFT):
                        last = pe.matmul(small[0][:, 0:P], w2_sb[:, j, :], gate[:, j, :],
                                         start=(j == 0), stop=(j == FFT - 1))
                    last.then_inc(p_w2, 1)
                if (n := on_tile(i, 0)) is not None:
                    pe.wait_ge(v_q, n + 1)
                    project(big[0], 2, layer_of(n)).then_inc(p_v, 1)
                if (n := on_tile(i, 4)) is not None:
                    pe.wait_ge(v_ysq, n + 1)
                    pe.matmul(small[1][:, 0:P], mean_w[:], ysq[:], start=True, stop=True).then_inc(p_var, 1)
                if (n := on_tile(i, 1)) is not None:
                    pe.wait_ge(a_kT, n + 1)
                    turn(big[2], rotn[:, 0]).then_inc(p_tq, 1)
                if (n := on_tile(i, 3)) is not None:
                    pe.wait_ge(a_oT, n + 1)
                    pe.wait_ge(w_o, (layer_of(n) + 1) * (NO * 16))
                    need(pe, v_x, n - 1)
                    for p in range(PAIRS):
                        last = pe.matmul(small[0][:, 0:P], wo_sb[:, p, :], oT[:, p, :],
                                         start=(p == 0), stop=(p == PAIRS - 1))
                    last.then_inc(p_wo, 1)
                if (n := on_tile(i, 2)) is not None:
                    pe.wait_ge(a_exp, n + 1)
                    pe.wait_ge(a_v, upto(i + 1))
                    need(pe, a_pT, n)
                    turn(big[0], prob).then_inc(p_pt, 1)
                if (n := on_tile(i, 1)) is not None:
                    pe.wait_ge(a_qT, n + 1)
                    pe.wait_ge(a_kT, n + 1)
                    pe.wait_ge(v_k, upto(i + 1))
                    need(pe, v_sub, i - 1)
                    first = ((n & (TILES - 1)) + TILES - 1) >> 4
                    if not isinstance(n, int):
                        first = first.with_bounds(min_val=0, max_val=1)
                    m = mask_b[:, bass.ds(first, 1), :].broadcast_to([P, PAIRS, KEYS])
                    for h in range(2):
                        pe.matmul(big[1][:, h * BANK:(h + 1) * BANK].rearrange("p (h k) -> p h k", k=KEYS),
                                  ident_b[:], m, start=True, stop=False, skip_group_check=True)
                    for p in range(PAIRS):
                        for c in range(NWIN):
                            rows = slice(c * WIN, (c + 1) * WIN)
                            last = pe.matmul(big[1][rows, p * P:(p + 1) * P], qT[:, p, rows],
                                             kT[:, p, :, c * WIN:c * WIN + KEYS], start=False, stop=True,
                                             skip_group_check=True)
                    last.then_inc(p_s, 1)
                if (n := on_tile(i, 4)) is not None:
                    pe.wait_ge(v_yn, n + 1)
                    pe.wait_ge(w_1, (layer_of(n) + 1) * (N1 * 16))
                    need(pe, v_y, upto(i - 2))
                    for ps, a, done in ((small[1], 1, p_gate), (small[0], 0, p_a)):
                        for j in range(FFT):
                            last = pe.matmul(ps[:, j * P:(j + 1) * P], w1_sb[:, a, j * P:(j + 1) * P], yn[:],
                                             start=True, stop=True)
                        last.then_inc(done, 1)
                if (n := on_tile(i, 2)) is not None:
                    pe.wait_ge(a_pT, n + 1)
                    pe.wait_ge(vmoved, (n + 1) * (NVM * 16))
                    pe.wait_ge(a_qT, upto(i))
                    need(pe, a_oT, upto(i - 2))
                    for p in range(PAIRS):
                        for c in range(NWIN):
                            rows = slice(c * WIN, (c + 1) * WIN)
                            last = pe.matmul(big[2][rows, p * P:(p + 1) * P], pT[:, p, rows], vwin[:, c, :, p, :],
                                             start=True, stop=True, skip_group_check=True)
                    last.then_inc(p_pv, 1)

            pipeline(pe, step)


def stage_e(nc, x, ident, X, att_scratch, out):
    with ExitStack() as ctx:
        def sem(name):
            return ctx.enter_context(nc.semaphore(name))

        xin = ctx.enter_context(nc.sbuf_tensor("xinE", [P, TILES, DIM], F32))
        att = ctx.enter_context(nc.sbuf_tensor("attE", [P, SEQ], F32))
        g = ctx.enter_context(nc.sbuf_tensor("gE", [P, SEQ], F32))
        z = ctx.enter_context(nc.sbuf_tensor("zE", [P, SEQ], F32))
        res = ctx.enter_context(nc.sbuf_tensor("resE", [P, TILES, DIM], F32))
        ps = ctx.enter_context(nc.psum_tensor("psE", [P, 4, BANK], F32))
        x_in, att_in, stored, a_g, v_z, p_z, v_res = (
            sem(n) for n in ("x_inE", "att_in", "storedE", "a_g", "v_z", "p_z", "v_res"))
        block = ctx.enter_context(nc.Block())

        @block.sync
        def _(sp):
            sp.dma_start(att[:], att_scratch).then_inc(att_in, 16)
            sp.dma_start(xin[:], x[0].rearrange("(t p) d -> p t d", p=P)).then_inc(x_in, 16)
            rows = out[0].rearrange("(t p) d -> p t d", p=P)
            for c in range(4):
                sp.wait_ge(v_res, c + 1)
                sp.dma_start(rows[:, 4 * c:4 * c + 4], res[:, 4 * c:4 * c + 4]).then_inc(stored, 16)
            sp.wait_ge(stored, 64)

        @block.scalar
        def _(act):
            for c in range(4):
                act.activation(g[:, c * BANK:(c + 1) * BANK], X[:, 1 + c * BANK:1 + (c + 1) * BANK],
                               ACT.Silu).then_inc(a_g, 1)

        @block.vector
        def _(dve):
            dve.wait_ge(att_in, 16)
            for c in range(4):
                cols = slice(c * BANK, (c + 1) * BANK)
                dve.wait_ge(a_g, c + 1)
                dve.tensor_tensor(z[:, cols], att[:, cols], g[:, cols], ALU.mult).then_inc(v_z, 1)
            dve.wait_ge(x_in, 16)
            for c in range(4):
                dve.wait_ge(p_z, c + 1)
                dve.tensor_tensor(res[:, 4 * c:4 * c + 4], ps[:, c, :].rearrange("p (t d) -> p t d", t=4),
                                  xin[:, 4 * c:4 * c + 4], ALU.add).then_inc(v_res, 1)

        @block.tensor
        def _(pe):
            for t in range(TILES):
                if t % 4 == 0:
                    pe.wait_ge(v_z, t // 4 + 1)
                last = pe.transpose(ps[:, t // 4, t % 4 * P:(t % 4 + 1) * P], z[:, t * P:(t + 1) * P], ident[:])
                if t % 4 == 3:
                    last.then_inc(p_z, 1)


def shape_tables():
    f = np.float32
    half = np.arange(0, HD, 2, dtype=f)
    inv_freq = (f(1) / f(10000) ** (half / f(HD))).astype(f)
    angle = np.arange(SEQ, dtype=f)[:, None] * inv_freq[None, :]
    angle = np.concatenate([angle, angle], -1).astype(np.float64)
    base = ((half + 0.4 * HD) / (1.4 * HD)).astype(f).astype(np.float64)
    base = np.concatenate([base, base])
    power = (np.arange(SEQ) % P - P // 2) / (WIN // 2)
    scale = base[None, :] ** power[:, None]
    sign = np.where(np.arange(HD) < HD // 2, -1.0, 1.0)
    cos, sin = np.cos(angle), np.sin(angle) * sign
    rope = np.stack([8.0 * cos * scale, 8.0 * sin * scale, cos / scale, sin / scale], 1)
    rope = rope.reshape(TILES, P, 4, HD).transpose(1, 0, 2, 3).astype(f)
    carry = np.tile(base ** (P / (WIN // 2)), 2).reshape(P, 1).astype(f)
    row, key = np.arange(P)[:, None] % WIN, np.arange(KEYS)[None, :]
    ok = (row <= key) & (key <= row + WIN)
    first = ok & ((np.arange(P)[:, None] >= WIN) | (key >= WIN))
    mask = np.where(np.stack([first, ok], 1), 0.0, -1e30).astype(f)
    return {"rope": np.ascontiguousarray(rope), "carry_scale": carry, "mask": mask, "eye": np.eye(P, dtype=f)}


_INS = ["L0_attn_x", "L0_attn_Wv", "L0_attn_Wk", "L0_attn_Wq", "L0_attn_Wo", "L0_attn_bo", "L0_ffn_Wqkv",
        "L0_ffn_q_scale", "L0_ffn_k_scale", "L0_ffn_Wo", "L0_ffn_ln_g", "L0_ffn_ln_b", "L0_ffn_W1", "L0_ffn_b1",
        "L0_ffn_W2", "L0_ffn_b2"]


def kernel(**inputs):
    import concourse.bacc as _bacc
    from concourse.bass_utils import run_bass_kernel_spmd as _run

    nc = _bacc.Bacc("TRN2", target_bir_lowering=False, num_devices=1)
    arrays, args = {}, []
    tables = shape_tables()
    for name in _INS + list(tables):
        a = np.ascontiguousarray(tables[name] if name in tables else inputs[name])
        arrays[f"in_{name}"] = a
        args.append(nc.dram_tensor(f"in_{name}", a.shape, mybir.dt.from_np(a.dtype), kind="ExternalInput").ap())
    out = nc.dram_tensor("out_0", (1, SEQ, DIM), F32, kind="ExternalOutput").ap()
    build(nc, *args, out)
    r = _run(nc, [arrays], core_ids=[0])
    return r.results[0]["out_0"]
```
